# Optimizing a Trainium2 kernel written in Bass

```python
import numpy as np
import jax
import jax.numpy as jnp

def _softmax(x, axis=-1):
    return jax.nn.softmax(x, axis=axis)

def _gelu(x):
    return jax.nn.gelu(x, approximate=True)

def _silu(x):
    return jax.nn.silu(x)

def _sigmoid(x):
    return jax.nn.sigmoid(x)

def _layernorm(x, axis=-1, eps=1e-05):
    m = jnp.mean(x, axis=axis, keepdims=True)
    v = jnp.var(x, axis=axis, keepdims=True)
    return (x - m) / jnp.sqrt(v + eps)

def _scatter_add(tgt, idx, src, axis=0):
    return tgt.at[idx].add(src)

def _segment_sum(src, seg, n):
    return jax.ops.segment_sum(src, seg, n)
kernel_name = 'mk_gnn_preln_d4_gnn_r32_9dce5c'

def setup_inputs(seed: int=0):
    np.random.seed(seed)
    _w = jnp.asarray

    def _rec_inputs():
        import jax
        import jax.numpy as jnp
        _gk = jax.random.key(seed)
        x = -0.0002117 + 1 * jax.random.normal(jax.random.fold_in(_gk, 1), (3125, 256), jnp.float32)
        _s = jax.random.randint(jax.random.fold_in(_gk, 2), (25000,), 0, 3125, jnp.int32)
        _d = jax.random.randint(jax.random.fold_in(_gk, 3), (25000,), 0, 3125, jnp.int32)
        _loop = jnp.arange(3125, dtype=jnp.int32)
        src = jnp.concatenate([_s, _d, _loop])
        dst = jnp.concatenate([_d, _s, _loop])
        _o = jnp.argsort(dst, stable=True)
        src = src[_o]
        dst = dst[_o]
        edge_type_8 = jax.random.randint(jax.random.fold_in(_gk, 14), (53125,), 0, 8, jnp.int32)
        edge_weight = jax.random.uniform(jax.random.fold_in(_gk, 15), (53125,), jnp.float32, 0.0, 1)
        return (x, src, dst, edge_type_8, edge_weight)
    x, src, dst, edge_type_8, edge_weight = _rec_inputs()

    def _L0_gnn_setup():
        import jax, jax.numpy as jnp
        import numpy as np
        N_NODES = 3125
        N_EDGES = 100000
        D_IN = 256
        D_OUT = 256
        key = jax.random.key(seed)
        k1, k2, k3, k4, k5 = jax.random.split(key, 5)
        x = jax.random.normal(k1, (N_NODES, D_IN), dtype=jnp.float32)
        weight = jax.random.normal(k2, (D_IN, D_OUT), dtype=jnp.float32) * (1.0 / np.sqrt(D_IN))
        edge_row = jax.random.randint(k3, (N_EDGES,), 0, N_NODES, dtype=jnp.int32)
        edge_col = jax.random.randint(k4, (N_EDGES,), 0, N_NODES, dtype=jnp.int32)
        edge_val = jax.random.uniform(k5, (N_EDGES,), dtype=jnp.float32)
        return {'x': x, 'weight': weight, 'edge_row': edge_row, 'edge_col': edge_col, 'edge_val': edge_val}
    _L0_gnn_all = _L0_gnn_setup()
    _L0_gnn_in = {k: v for k, v in _L0_gnn_all.items() if k in ('weight',)}
    del _L0_gnn_all

    def _L1_gnn_setup():
        import jax, jax.numpy as jnp
        import numpy as np
        N_NODES = 50000
        N_EDGES = 25000
        IN_FEAT = 256
        OUT_FEAT = 256
        NUM_RELS = 8
        NUM_BASES = 8
        SUBMAT_IN = IN_FEAT // NUM_BASES
        SUBMAT_OUT = OUT_FEAT // NUM_BASES
        key = jax.random.key(seed)
        k_h, k_w, k_src, k_dst, k_rel, k_norm = jax.random.split(key, 6)
        h = jax.random.normal(k_h, (N_NODES, IN_FEAT), dtype=jnp.float32)
        weight = jax.random.normal(k_w, (NUM_RELS, NUM_BASES * SUBMAT_IN * SUBMAT_OUT), dtype=jnp.float32) * 0.05
        edge_src = jax.random.randint(k_src, (N_EDGES,), 0, N_NODES, dtype=jnp.int32)
        edge_dst = jax.random.randint(k_dst, (N_EDGES,), 0, N_NODES, dtype=jnp.int32)
        edge_rel = jax.random.randint(k_rel, (N_EDGES,), 0, NUM_RELS, dtype=jnp.int32)
        edge_norm = jax.random.uniform(k_norm, (N_EDGES,), dtype=jnp.float32)
        return {'h': h, 'weight': weight, 'edge_src': edge_src, 'edge_dst': edge_dst, 'edge_rel': edge_rel, 'edge_norm': edge_norm}
    _L1_gnn_all = _L1_gnn_setup()
    _L1_gnn_in = {k: v for k, v in _L1_gnn_all.items() if k in ('weight',)}
    del _L1_gnn_all

    def _L2_gnn_setup():
        import jax, jax.numpy as jnp
        import numpy as np
        N, E = (50000, 25000)
        IN_DIM = 256
        OUT_DIM = 256
        H = 8
        D = OUT_DIM // H
        SCALE = D ** (-0.5)
        LN_EPS = 1e-05

        def _layernorm(x, g, b):
            mu = jnp.mean(x, axis=-1, keepdims=True)
            var = jnp.mean((x - mu) ** 2, axis=-1, keepdims=True)
            return (x - mu) * jax.lax.rsqrt(var + LN_EPS) * g + b
        key = jax.random.key(seed)
        ks = jax.random.split(key, 12)
        s = 1.0 / np.sqrt(IN_DIM)
        inp = {'x': jax.random.normal(ks[0], (N, IN_DIM), jnp.float32), 'edge_index': jax.random.randint(ks[1], (2, E), 0, N, jnp.int64), 'batch': jnp.zeros((N,), jnp.int64), 'Wq': jax.random.uniform(ks[2], (IN_DIM, OUT_DIM), jnp.float32, -s, s), 'Wk': jax.random.uniform(ks[3], (IN_DIM, OUT_DIM), jnp.float32, -s, s), 'Wv': jax.random.uniform(ks[4], (IN_DIM, OUT_DIM), jnp.float32, -s, s), 'Wo_w': jax.random.uniform(ks[5], (OUT_DIM, OUT_DIM), jnp.float32, -s, s), 'Wo_b': jnp.zeros((OUT_DIM,), jnp.float32), 'ln1_g': jnp.ones((OUT_DIM,), jnp.float32), 'ln1_b': jnp.zeros((OUT_DIM,), jnp.float32), 'ln2_g': jnp.ones((OUT_DIM,), jnp.float32), 'ln2_b': jnp.zeros((OUT_DIM,), jnp.float32), 'ffn_w1': jax.random.uniform(ks[6], (OUT_DIM, 2 * OUT_DIM), jnp.float32, -s, s), 'ffn_b1': jnp.zeros((2 * OUT_DIM,), jnp.float32), 'ffn_w2': jax.random.uniform(ks[7], (2 * OUT_DIM, OUT_DIM), jnp.float32, -s, s), 'ffn_b2': jnp.zeros((OUT_DIM,), jnp.float32)}
        return inp
    _L2_gnn_all = _L2_gnn_setup()
    _L2_gnn_in = {k: v for k, v in _L2_gnn_all.items() if k in ('Wq', 'Wk', 'Wv', 'Wo_w', 'Wo_b', 'ln1_g', 'ln1_b', 'ln2_g', 'ln2_b', 'ffn_w1', 'ffn_b1', 'ffn_w2', 'ffn_b2')}
    del _L2_gnn_all

    def _L3_gnn_setup():
        import jax, jax.numpy as jnp
        import numpy as np
        ALPHA = 0.2
        N_NODES, N_EDGES, N_FEAT, N_HID, N_HEADS = (50000, 25000, 256, 32, 8)
        key = jax.random.key(seed)
        k_h, k_w, k_a, k_s, k_d = jax.random.split(key, 5)
        h = jax.random.normal(k_h, (N_NODES, N_FEAT), dtype=jnp.float32)
        W = jax.random.normal(k_w, (N_HEADS, N_FEAT, N_HID), dtype=jnp.float32) * 0.05
        a = jax.random.normal(k_a, (N_HEADS, 2 * N_HID), dtype=jnp.float32) * 0.05
        src = jax.random.randint(k_s, (N_EDGES,), 0, N_NODES, dtype=jnp.int32)
        dst = jax.random.randint(k_d, (N_EDGES,), 0, N_NODES, dtype=jnp.int32)
        return {'h': h, 'W': W, 'a': a, 'src': src, 'dst': dst}
    _L3_gnn_all = _L3_gnn_setup()
    _L3_gnn_in = {k: v for k, v in _L3_gnn_all.items() if k in ('W', 'a')}
    del _L3_gnn_all
    return {'x': x, 'src': src, 'dst': dst, 'edge_type_8': edge_type_8, 'edge_weight': edge_weight, 'L0_gnn_weight': _L0_gnn_in['weight'], 'L1_gnn_weight': _L1_gnn_in['weight'], 'L2_gnn_Wq': _L2_gnn_in['Wq'], 'L2_gnn_Wk': _L2_gnn_in['Wk'], 'L2_gnn_Wv': _L2_gnn_in['Wv'], 'L2_gnn_Wo_w': _L2_gnn_in['Wo_w'], 'L2_gnn_Wo_b': _L2_gnn_in['Wo_b'], 'L2_gnn_ln1_g': _L2_gnn_in['ln1_g'], 'L2_gnn_ln1_b': _L2_gnn_in['ln1_b'], 'L2_gnn_ln2_g': _L2_gnn_in['ln2_g'], 'L2_gnn_ln2_b': _L2_gnn_in['ln2_b'], 'L2_gnn_ffn_w1': _L2_gnn_in['ffn_w1'], 'L2_gnn_ffn_b1': _L2_gnn_in['ffn_b1'], 'L2_gnn_ffn_w2': _L2_gnn_in['ffn_w2'], 'L2_gnn_ffn_b2': _L2_gnn_in['ffn_b2'], 'L3_gnn_W': _L3_gnn_in['W'], 'L3_gnn_a': _L3_gnn_in['a']}

def reference(x, src, dst, edge_type_8, edge_weight, L0_gnn_weight, L1_gnn_weight, L2_gnn_Wq, L2_gnn_Wk, L2_gnn_Wv, L2_gnn_Wo_w, L2_gnn_Wo_b, L2_gnn_ln1_g, L2_gnn_ln1_b, L2_gnn_ln2_g, L2_gnn_ln2_b, L2_gnn_ffn_w1, L2_gnn_ffn_b1, L2_gnn_ffn_w2, L2_gnn_ffn_b2, L3_gnn_W, L3_gnn_a):
    import jax
    import jax.numpy as jnp

    def _L0_gnn_ref(x, weight, edge_row, edge_col, edge_val):
        import jax, jax.numpy as jnp
        import numpy as np
        N_NODES = 3125
        N_EDGES = 100000
        D_IN = 256
        D_OUT = 256
        support = x @ weight
        gathered = edge_val[:, None] * support[edge_col]
        output = jax.ops.segment_sum(gathered, edge_row, num_segments=N_NODES)
        return output

    def _L1_gnn_ref(h, weight, edge_src, edge_dst, edge_rel, edge_norm):
        import jax, jax.numpy as jnp
        import numpy as np
        N_NODES = 50000
        N_EDGES = 25000
        IN_FEAT = 256
        OUT_FEAT = 256
        NUM_RELS = 8
        NUM_BASES = 8
        SUBMAT_IN = IN_FEAT // NUM_BASES
        SUBMAT_OUT = OUT_FEAT // NUM_BASES
        'RGCNBlockLayer forward (self_loop=False, bias=None, activation=None).\n\n            Per relation r: agg_r[v] = sum_{(u->v) in rel r} norm_e * h[u]\n            then block-diagonal matmul out_r = blockmm(agg_r, W_r); output = sum_r out_r.\n            '
        N, in_feat = h.shape
        R = weight.shape[0]
        msg = h[edge_src] * edge_norm[:, None]
        seg = edge_rel * N + edge_dst
        agg = jax.ops.segment_sum(msg, seg, num_segments=R * N)
        agg = agg.reshape(R, N, NUM_BASES, SUBMAT_IN)
        W = weight.reshape(R, NUM_BASES, SUBMAT_IN, SUBMAT_OUT)
        out = jnp.einsum('rnbi,rbio->nbo', agg, W)
        return out.reshape(N, NUM_BASES * SUBMAT_OUT)

    def _L2_gnn_ref(x, edge_index, batch, Wq, Wk, Wv, Wo_w, Wo_b, ln1_g, ln1_b, ln2_g, ln2_b, ffn_w1, ffn_b1, ffn_w2, ffn_b2):
        import jax, jax.numpy as jnp
        import numpy as np
        N, E = (50000, 25000)
        IN_DIM = 256
        OUT_DIM = 256
        H = 8
        D = OUT_DIM // H
        SCALE = D ** (-0.5)
        LN_EPS = 1e-05

        def _layernorm(x, g, b):
            mu = jnp.mean(x, axis=-1, keepdims=True)
            var = jnp.mean((x - mu) ** 2, axis=-1, keepdims=True)
            return (x - mu) * jax.lax.rsqrt(var + LN_EPS) * g + b
        n = x.shape[0]
        residual = x
        Q = (x @ Wq).reshape(n, H, D)
        K = (x @ Wk).reshape(n, H, D)
        V = (x @ Wv).reshape(n, H, D)
        src, dst = (edge_index[0], edge_index[1])
        scores = jnp.einsum('ehd,ehd->eh', Q[dst], K[src]) * SCALE
        attn_max = jnp.zeros((n, H), scores.dtype).at[dst].max(scores)
        w = jnp.exp(scores - attn_max[dst])
        attn_sum = jnp.zeros((n, H), w.dtype).at[dst].add(w)
        w = w / (attn_sum[dst] + 1e-08)
        msg = V[src] * w[:, :, None]
        out = jnp.zeros((n, H, D), msg.dtype).at[dst].add(msg)
        out = out.reshape(n, OUT_DIM) @ Wo_w + Wo_b
        out = _layernorm(residual + out, ln1_g, ln1_b)
        ffn = jax.nn.gelu(out @ ffn_w1 + ffn_b1, approximate=False) @ ffn_w2 + ffn_b2
        out = _layernorm(out + ffn, ln2_g, ln2_b)
        return out

    def _L3_gnn_ref(h, W, a, src, dst):
        import jax, jax.numpy as jnp
        import numpy as np
        ALPHA = 0.2
        N_NODES, N_EDGES, N_FEAT, N_HID, N_HEADS = (50000, 25000, 256, 32, 8)
        N = h.shape[0]
        H, _, D = W.shape
        Wh = jnp.einsum('nf,hfd->hnd', h, W)
        a1, a2 = (a[:, :D], a[:, D:])
        s1 = jnp.einsum('hnd,hd->hn', Wh, a1)
        s2 = jnp.einsum('hnd,hd->hn', Wh, a2)
        e = jax.nn.leaky_relu(s1[:, src] + s2[:, dst], ALPHA)
        seg_max = jax.vmap(lambda x: jax.ops.segment_max(x, dst, num_segments=N))(e)
        ex = jnp.exp(e - seg_max[:, dst])
        denom = jax.vmap(lambda x: jax.ops.segment_sum(x, dst, num_segments=N))(ex)
        attn = ex / denom[:, dst]
        msg = attn[:, :, None] * Wh[:, src]
        out = jax.vmap(lambda m: jax.ops.segment_sum(m, dst, num_segments=N))(msg)
        return jnp.transpose(out, (1, 0, 2)).reshape(N, H * D)
    edge_index = jnp.stack([src, dst])
    batch0 = jnp.zeros((3125,), jnp.int32)
    h = jnp.maximum(_layernorm(x, axis=-1), 0.0)
    x = x + _L0_gnn_ref(h, L0_gnn_weight, src, dst, edge_weight)
    h = jnp.maximum(_layernorm(x, axis=-1), 0.0)
    x = x + _L1_gnn_ref(h, L1_gnn_weight, src, dst, edge_type_8, edge_weight)
    h = jnp.maximum(_layernorm(x, axis=-1), 0.0)
    x = x + _L2_gnn_ref(h, edge_index, batch0, L2_gnn_Wq, L2_gnn_Wk, L2_gnn_Wv, L2_gnn_Wo_w, L2_gnn_Wo_b, L2_gnn_ln1_g, L2_gnn_ln1_b, L2_gnn_ln2_g, L2_gnn_ln2_b, L2_gnn_ffn_w1, L2_gnn_ffn_b1, L2_gnn_ffn_w2, L2_gnn_ffn_b2)
    h = jnp.maximum(_layernorm(x, axis=-1), 0.0)
    x = x + _L3_gnn_ref(h, L3_gnn_W, L3_gnn_a, src, dst)
    return x

_drawn_inputs = setup_inputs


def setup_inputs(seed=0):
    import zlib

    import numpy as np

    out = dict(_drawn_inputs(seed))
    spreads = {'L2_gnn_Wo_b': (0.0, 0.277),
     'L2_gnn_ln1_g': (1.0, 0.2),
     'L2_gnn_ln1_b': (0.0, 0.406),
     'L2_gnn_ln2_g': (1.0, 0.2),
     'L2_gnn_ln2_b': (0.0, 0.364),
     'L2_gnn_ffn_b1': (0.0, 0.782),
     'L2_gnn_ffn_b2': (0.0, 0.368)}
    factors = {'L2_gnn_Wq': 8.0, 'L2_gnn_Wk': 8.0, 'L3_gnn_a': 48.144}
    for name, (base, spread) in spreads.items():
        noise = np.random.default_rng([zlib.crc32(name.encode()), seed]).standard_normal(out[name].shape)
        drawn = base * np.exp(spread * noise) if base else spread * noise
        out[name] = jnp.asarray(drawn.astype(out[name].dtype))
    for name, factor in factors.items():
        out[name] = (out[name] * factor).astype(out[name].dtype)
    return out
```

```python
from contextlib import ExitStack

import concourse.bass as bass
from concourse import mybir
from concourse.alu_op_type import AluOpType as ALU

ACT = mybir.ActivationFunctionType
AX = mybir.AxisListType
F32 = mybir.dt.float32
I32 = mybir.dt.int32
BF16 = mybir.dt.bfloat16

P = 128
N = 3125
D = 256
E = 53125
H = 8
DH = D // H
NP = 125
NT = N // NP
NTP = NT + 1
EC = -(-E // P)
ET = EC + NT - 1
G = 5
NG = 4
ITER = ET // (G * NG)
CH = 16
CT = -(-ET // CH)
SQ = CH * CT
CE = CT * P
MAGIC = 12582912.0
BIG = 1e30
SCALE = DH ** -0.5
EPS = 1e-5
T = G * NG
MW = D + H
assert ET == ITER * G * NG and N == NT * NP




class Link:

    def __init__(self, eng, sem):
        self.eng, self.sem, self.n = eng, sem, 0

    def __call__(self, ins):
        self.n += 1
        ins.then_inc(self.sem, 1)
        self.eng.wait_ge(self.sem, self.n)


def build(nc, x, src, dst, edge_type_8, edge_weight, L0_gnn_weight, L1_gnn_weight, L2_gnn_Wq, L2_gnn_Wk,
          L2_gnn_Wv, L2_gnn_Wo_w, L2_gnn_Wo_b, L2_gnn_ln1_g, L2_gnn_ln1_b, L2_gnn_ln2_g, L2_gnn_ln2_b,
          L2_gnn_ffn_w1, L2_gnn_ffn_b1, L2_gnn_ffn_w2, L2_gnn_ffn_b2, L3_gnn_W, L3_gnn_a, out, stop_after=99, dbg=None):
    top = ExitStack()

    def dram(name, shape):
        return nc.dram_tensor(name, shape, F32, kind="Internal").ap()

    edges = dram("edges", [EC, P * 4])
    dst_seq = dram("dst_seq", [P + SQ * P + CE])
    ldst_seq = dram("ldst_seq", [ET * P])
    by_src = dram("by_src", [ET * P, MW])
    rel_table = dram("rel_table", [NTP * NP * H, D])
    key_table = dram("key_table", [NTP * NP, D])
    value_table = dram("value_table", [NTP * NP, D])
    wh_table = dram("wh_table", [NTP * NP, D])
    s1_table = dram("s1_table", [NTP * NP, H])
    score_rows = dram("score_rows", [SQ * H, P])
    prob_rows = dram("prob_rows", [SQ * H, P])

    with top:
        def sb(ctx, name, shape, dt=F32):
            return ctx.enter_context(nc.sbuf_tensor(name, shape, dt))

        def ps(ctx, name, shape):
            return ctx.enter_context(nc.psum_tensor(name, shape, F32))

        held = {}

        def sem(ctx, name):
            if ctx not in held:
                held[ctx] = []
                ctx.callback(clear, ctx)
            held[ctx].append(nc.alloc_semaphore(name=name))
            return held[ctx][-1]

        def clear(ctx):
            nc.all_engine_barrier()
            nc.clear_and_free_semaphores(held.pop(ctx))
            nc.all_engine_barrier()

        X = sb(top, "X", [NP, NTP, D])
        acc = sb(top, "acc", [NP, NTP, MW])
        table = sb(top, "table", [NP, NTP, D])
        ident = sb(top, "ident", [P, P])
        iota_f = sb(top, "iota_f", [P, P])
        iota_p = sb(top, "iota_p", [P, 1])
        ones = sb(top, "ones", [P, P])
        own_s = sb(top, "own_s", [1, ET], I32)
        own_d = sb(top, "own_d", [1, ET], I32)
        meta = sb(top, "meta", [P, ET, 4])
        rel_idx = sb(top, "rel_idx", [P, ET], I32)
        src_idx = sb(top, "src_idx", [P, ET + T], I32)
        slot_idx = sb(top, "slot_idx", [P, ET], I32)
        ldst = sb(top, "ldst", [P, ET])
        lsrc = sb(top, "lsrc", [P, ET])
        rstd = sb(top, "rstd", [NP, NTP])
        nmr = sb(top, "nmr", [NP, NTP])

        def constants_and_edges():
            with ExitStack() as c:
                srcn, dstn, typn = (sb(c, n, [P, EC], I32) for n in ("srcn", "dstn", "typn"))
                srcf, dstf, typf, wgt, bins, bind, eq, cum, tmp, tmp2, rank = (
                    sb(c, n, [P, EC]) for n in "srcf dstf typf wgt bins bind eq cum tmp tmp2 rank".split())
                mark = sb(c, "mark", [1, 1])
                rows = sb(c, "rows", [P, EC, 4])
                padseq = sb(c, "padseq", [P, P])
                before = sb(c, "before", [P, P])
                upto = sb(c, "upto", [P, P])
                iota_j = sb(c, "iota_j", [P, ET])
                cnt = sb(c, "cnt", [P, 2, NT])
                tiles_of = sb(c, "tiles_of", [P, NT])
                tiles_end = sb(c, "tiles_end", [P, NT])
                first = sb(c, "first", [P, NT])
                cols = sb(c, "cols", [NT, 8])
                ge_s, ge_d = sb(c, "ge_s", [NT, ET]), sb(c, "ge_d", [NT, ET])
                zero = sb(c, "zero", [P, MW])
                p_small = ps(c, "p_small", [P, 512])
                p_col = ps(c, "p_col", [P, 512])
                p_own_s = ps(c, "p_own_s", [P, 512])
                p_own_d = ps(c, "p_own_d", [P, 512])
                p_tr = ps(c, "p_tr", [P, 4, P])
                p_meta = [ps(c, f"p_meta{i}", [P, 4, P]) for i in range(2)]
                q = ET // 4
                blocks = sb(c, "blocks", [q, 4, P * 4])
                block_of = sb(c, "block_of", [q, 4], I32)
                block_f = sb(c, "block_f", [q, 4])
                tile_no = sb(c, "tile_no", [q, 4])
                pad_f = sb(c, "pad_f", [P, 2 * NT])
                pad_ok = sb(c, "pad_ok", [P, NT])
                pads = sb(c, "pads", [P, 2 * NT], I32)
                own_rep = sb(c, "own_rep", [P, ET])
                srce, owned, work, dst_of = (sb(c, n, [P, ET]) for n in "srce owned work dst_of".split())
                seqt = sb(c, "seqt", [ET // 4, 2, 4, P])
                (s_set, s_in, s_const, s_ch, s_pe, s_cnt, s_end, s_rows, s_seq, s_x, s_blk, s_off, s_ready, s_tr, s_trc,
                 s_fill, s_m, s_mc, s_pads, s_padded) = (sem(c, "e_" + n) for n in
                            "set in const ch pe cnt end rows seq x blk off ready tr trc fill m mc pads padded".split())

                with nc.Block() as block:
                    @block.gpsimd
                    def _(pool):
                        g = nc.gpsimd
                        k = Link(pool, s_const)
                        exact = dict(allow_small_or_imprecise_dtypes=True)
                        k(g.iota(iota_f[:, :], [[1, P]], base=0, channel_multiplier=0, **exact))
                        k(g.iota(iota_p[:, :], [[0, 1]], base=0, channel_multiplier=1, **exact))
                        k(g.iota(iota_j[:, :], [[1, ET]], base=0, channel_multiplier=0, **exact))
                        k(g.iota(tile_no[:, :], [[q, 4]], base=0, channel_multiplier=1, **exact))
                        k(g.memset(ident[:, :], 0.0))
                        k(g.memset(ones[:, :], 1.0))
                        k(g.affine_select(out=before[:, :], in_=ones[:, :], pattern=[[1, P]], compare_op=ALU.is_gt,
                                          fill=0.0, base=0, channel_multiplier=-1))
                        k(g.affine_select(out=upto[:, :], in_=ones[:, :], pattern=[[1, P]], compare_op=ALU.is_ge,
                                          fill=0.0, base=0, channel_multiplier=-1))
                        k(g.affine_select(out=ident[:, :], in_=ident[:, :], pattern=[[1, P]], compare_op=ALU.not_equal,
                                          fill=1.0, base=0, channel_multiplier=-1))
                        pool.wait_ge(s_off, 1)
                        pool.wait_ge(s_rows, 16)
                        for i in range(4):
                            g.indirect_dma_start(blocks[:, i, :], None, edges,
                                                 bass.IndirectOffsetOnAxis(ap=block_of[:, i:i + 1], axis=0)).then_inc(s_blk, 16)
                        pool.wait_ge(s_pads, 1)
                        for i in range(2 * NT):
                            g.indirect_dma_start(by_src, bass.IndirectOffsetOnAxis(ap=pads[:, i:i + 1], axis=0), zero[:, :], None,
                                                 bounds_check=ET * P - 1, oob_is_err=False).then_inc(s_padded, 16)
                        pool.wait_ge(s_padded, 16 * 2 * NT)

                    @block.sync
                    def _(sp):
                        last = (P - 1) * EC
                        sp.wait_ge(s_set, 1)
                        for a, t in ((src, srcn), (dst, dstn), (edge_type_8, typn), (edge_weight, wgt)):
                            sp.dma_start(t[0:P - 1, :], a[0:last].rearrange("(p e) -> p e", e=EC)).then_inc(s_in, 16)
                            sp.dma_start(t[P - 1:P, 0:E - last], a[last:E].rearrange("(p e) -> p e", p=1)).then_inc(s_in, 16)
                        sp.dma_start(X[:, 0:NT, :], x.rearrange("(t p) f -> p t f", p=NP)).then_inc(s_x, 16)
                        sp.dma_start(dst_seq[0:P].rearrange("(p e) -> p e", p=1), padseq[0:1, :]).then_inc(s_seq, 16)
                        tail = SQ - ET + 1
                        sp.dma_start(dst_seq[P + ET * P:P + ET * P + tail * P].rearrange("(p e) -> p e", e=P),
                                     padseq[0:tail, :]).then_inc(s_seq, 16)
                        sp.dma_start(score_rows[ET * H:SQ * H, :], zero[0:(SQ - ET) * H, 0:P]).then_inc(s_seq, 16)
                        sp.wait_ge(s_fill, 1)
                        sp.dma_start(edges.rearrange("b (e f) -> (b e f)", f=4).rearrange("(p w) -> p w", p=P),
                                     rows[:, :, :].rearrange("p e f -> p (e f)")).then_inc(s_rows, 16)
                        for k, seq, at in ((0, dst_seq, P), (1, ldst_seq, 0)):
                            sp.wait_ge(s_trc, k + 1)
                            for i in range(4):
                                sp.dma_start(seq[at + i * q * P:at + (i + 1) * q * P].rearrange("(p e) -> p e", e=P),
                                             seqt[:, k, i, :]).then_inc(s_seq, 16)
                        sp.wait_ge(s_x, 16)
                        sp.wait_ge(s_seq, 16 * (3 + 8))

                    @block.tensor
                    def _(pe):
                        mm = nc.tensor.matmul
                        pe.wait_ge(s_const, 9)
                        pe.wait_ge(s_cnt, 1)
                        mm(p_small[:, 0:NT], before[:, :], cnt[:, 0, :], start=True, stop=True)
                        mm(p_small[:, 32:32 + NT], ones[:, :], cnt[:, 0, :], start=True, stop=True)
                        mm(p_col[0:NT, 0:1], cnt[:, 0, :], ones[:, 0:1], start=True, stop=True)
                        mm(p_col[0:NT, 1:2], cnt[:, 1, :], ones[:, 0:1], start=True, stop=True).then_inc(s_pe, 1)
                        pe.wait_ge(s_end, 1)
                        mm(p_col[0:NT, 4:5], before[0:NT, 0:NT], cols[:, 1:2], start=True, stop=True).then_inc(s_pe, 1)
                        pe.wait_ge(s_end, 2)
                        mm(p_col[0:NT, 2:4], upto[0:NT, 0:NT], cols[:, 2:4], start=True, stop=True).then_inc(s_pe, 1)
                        pe.wait_ge(s_end, 3)
                        for i in range(4):
                            mm(p_col[0:q, 8 + i:9 + i], ge_d[:, i * q:(i + 1) * q], cols[:, 4:5], start=True, stop=True)
                        mm(p_own_s[:, 0:ET], ones[0:NT, :], ge_s[:, :], start=True, stop=True)
                        mm(p_own_d[:, 0:ET], ones[0:NT, :], ge_d[:, :], start=True, stop=True).then_inc(s_pe, 1)
                        pe.wait_ge(s_blk, 64)
                        for i in range(4):
                            if i >= 2:
                                pe.wait_ge(s_mc, i - 1)
                            for f in range(4):
                                ins = nc.tensor.transpose(p_meta[i % 2][:, f, 0:q], blocks[:, i, f:P * 4:4], ident[0:q, 0:q])
                            ins.then_inc(s_m, 1)
                        for k, a in ((0, dst_of), (1, ldst)):
                            pe.wait_ge(s_ready, 1)
                            if k:
                                pe.wait_ge(s_trc, 1)
                            for i in range(4):
                                ins = nc.tensor.transpose(p_tr[0:q, i, :], a[:, i * q:(i + 1) * q], ident[:, :])
                            ins.then_inc(s_tr, 1)

                    @block.vector
                    def _(dve):
                        v = nc.vector
                        go = Link(dve, s_ch)
                        go(v.memset(srcn[:, :], 4095))
                        go(v.memset(dstn[:, :], 4095))
                        go(v.memset(typn[:, :], 0))
                        go(v.memset(wgt[:, :], 0.0))
                        go(v.memset(padseq[:, :], -1.0))
                        go(v.memset(zero[:, 0:D], 0.0))
                        v.memset(zero[:, D:MW], -1.0).then_inc(s_set, 1)
                        dve.wait_ge(s_set, 1)
                        go(v.memset(X[:, NT, :], 0.0))
                        go(v.memset(acc[:, :, :], 0.0))
                        go(v.memset(rank[:, :], 0.0))
                        dve.wait_ge(s_in, 16 * 8)
                        dve.wait_ge(s_const, 9)
                        go(v.tensor_copy(srcf[:, :], srcn[:, :]))
                        go(v.tensor_copy(dstf[:, :], dstn[:, :]))
                        go(v.tensor_copy(typf[:, :], typn[:, :]))
                        for f, b in ((srcf, bins), (dstf, bind)):
                            go(v.tensor_scalar(b[:, :], f[:, :], 1.0 / NP, -(NP // 2) / NP, ALU.mult, ALU.add))
                            go(v.tensor_scalar(b[:, :], b[:, :], MAGIC, -MAGIC, ALU.add, ALU.add))
                        go(v.scalar_tensor_tensor(out=tmp[:, :], in0=srcf[:, :], scalar=float(H), in1=typf[:, :],
                                                  op0=ALU.mult, op1=ALU.add))
                        go(v.tensor_scalar(rows[:, :, 0], tmp[:, :], float(N * H - 1), None, ALU.min))
                        go(v.tensor_copy(rows[:, :, 1], dstf[:, :]))
                        go(v.tensor_copy(rows[:, :, 2], wgt[:, :]))
                        go(v.memset(typf[:, :], 1.0))
                        n0 = go.n
                        with dve.Fori(0, NT) as b:
                            at = b * 6 + n0
                            tile = iota_f[:, bass.ds(b, 1)]
                            v.tensor_scalar(eq[:, :], bins[:, :], tile, None, ALU.is_equal).then_inc(s_ch, 1)
                            v.tensor_scalar(tmp2[:, :], bind[:, :], tile, 0.0, ALU.is_equal, ALU.add,
                                            accum_out=cnt[:, 1, bass.ds(b, 1)]).then_inc(s_ch, 1)
                            dve.wait_ge(s_ch, at + 2)
                            v.tensor_tensor_scan(cum[:, :], typf[:, :], eq[:, :], 0.0, ALU.mult, ALU.add).then_inc(s_ch, 1)
                            dve.wait_ge(s_ch, at + 3)
                            v.tensor_copy(cnt[:, 0, bass.ds(b, 1)], cum[:, EC - 1:EC]).then_inc(s_ch, 1)
                            v.tensor_tensor(tmp[:, :], eq[:, :], cum[:, :], ALU.mult).then_inc(s_ch, 1)
                            dve.wait_ge(s_ch, at + 5)
                            v.tensor_tensor(rank[:, :], rank[:, :], tmp[:, :], ALU.add).then_inc(s_ch, 1)
                            dve.wait_ge(s_ch, at + 6)
                        go.n = n0 + NT * 6
                        v.memset(mark[:, :], 0.0).then_inc(s_cnt, 1)
                        dve.wait_ge(s_cnt, 1)
                        dve.wait_ge(s_pe, 1)
                        up = (P - 1) / 2 / P
                        go(v.tensor_copy(cols[:, 0:2], p_col[0:NT, 0:2]))
                        go(v.tensor_scalar(cols[:, 2:3], cols[:, 0:1], 1.0 / P, up, ALU.mult, ALU.add))
                        v.tensor_scalar(cols[:, 2:3], cols[:, 2:3], MAGIC, -MAGIC, ALU.add, ALU.add).then_inc(s_end, 1)
                        dve.wait_ge(s_end, 1)
                        dve.wait_ge(s_pe, 2)
                        go(v.tensor_copy(cols[:, 5:6], p_col[0:NT, 4:5]))
                        go(v.tensor_tensor(cols[:, 6:7], cols[:, 5:6], cols[:, 1:2], ALU.add))
                        go(v.tensor_scalar(cols[:, 7:8], cols[:, 6:7], -1.0, None, ALU.add))
                        go(v.tensor_scalar(cols[:, 5:8], cols[:, 5:8], 1.0 / P, -up, ALU.mult, ALU.add))
                        go(v.tensor_scalar(cols[:, 5:8], cols[:, 5:8], MAGIC, -MAGIC, ALU.add, ALU.add))
                        go(v.tensor_tensor(cols[:, 3:4], cols[:, 7:8], cols[:, 5:6], ALU.subtract))
                        go(v.tensor_scalar(cols[:, 3:4], cols[:, 3:4], 1.0, None, ALU.add))
                        go(v.tensor_scalar(cols[:, 7:8], cols[:, 1:2], 0.0, None, ALU.is_gt))
                        go(v.tensor_tensor(cols[:, 3:4], cols[:, 3:4], cols[:, 7:8], ALU.mult))
                        go(v.tensor_tensor(cols[:, 4:5], cols[:, 6:7], cols[:, 5:6], ALU.subtract))
                        v.tensor_tensor(cols[:, 4:5], cols[:, 4:5], cols[:, 3:4], ALU.subtract).then_inc(s_end, 1)
                        dve.wait_ge(s_end, 2)
                        dve.wait_ge(s_pe, 3)
                        go(v.tensor_copy(cols[:, 6:8], p_col[0:NT, 2:4]))
                        go(v.tensor_scalar(ge_s[:, :], iota_j[0:NT, :], cols[:, 6:7], None, ALU.is_ge))
                        v.tensor_scalar(ge_d[:, :], iota_j[0:NT, :], cols[:, 7:8], None, ALU.is_ge).then_inc(s_end, 1)
                        dve.wait_ge(s_end, 3)
                        go(v.tensor_scalar(tiles_of[:, :], p_small[:, 32:32 + NT], 1.0 / P, up, ALU.mult, ALU.add))
                        go(v.tensor_scalar(tiles_of[:, :], tiles_of[:, :], MAGIC, -MAGIC, ALU.add, ALU.add))
                        go(v.tensor_tensor_scan(tiles_end[:, :], typf[:, 0:NT], tiles_of[:, :], 0.0, ALU.mult, ALU.add))
                        go(v.tensor_tensor(first[:, :], tiles_end[:, :], tiles_of[:, :], ALU.subtract))
                        go(v.tensor_scalar(first[:, :], first[:, :], float(P), -1.0, ALU.mult, ALU.add))
                        go(v.tensor_tensor(first[:, :], first[:, :], p_small[:, 0:NT], ALU.add))
                        n1 = go.n
                        with dve.Fori(0, NT) as b:
                            v.tensor_scalar(tmp[:, :], bins[:, :], iota_f[:, bass.ds(b, 1)], first[:, bass.ds(b, 1)],
                                            ALU.is_equal, ALU.mult).then_inc(s_ch, 1)
                            dve.wait_ge(s_ch, b * 2 + (n1 + 1))
                            v.tensor_tensor(rank[:, :], rank[:, :], tmp[:, :], ALU.add).then_inc(s_ch, 1)
                            dve.wait_ge(s_ch, b * 2 + (n1 + 2))
                        go.n = n1 + 2 * NT
                        v.tensor_copy(rows[:, :, 3], rank[:, :]).then_inc(s_fill, 1)
                        dve.wait_ge(s_pe, 4)
                        go(v.tensor_tensor(block_f[:, :], tile_no[:, :], p_col[0:q, 8:12], ALU.add))
                        v.tensor_scalar(block_of[:, :], block_f[:, :], float(EC - 1), None, ALU.min).then_inc(s_off, 1)
                        go(v.tensor_copy(own_s[:, :], p_own_s[0:1, 0:ET]))
                        go(v.tensor_copy(own_d[:, :], p_own_d[0:1, 0:ET]))
                        go(v.tensor_copy(own_rep[:, :], p_own_d[:, 0:ET]))
                        go(v.tensor_scalar(pad_f[:, 0:NT], tiles_end[:, :], float(P), float(-P), ALU.mult, ALU.add))
                        go(v.tensor_scalar(pad_f[:, 0:NT], pad_f[:, 0:NT], iota_p[:, :], None, ALU.add))
                        go(v.tensor_tensor(tiles_of[:, :], tiles_end[:, :], tiles_of[:, :], ALU.subtract))
                        go(v.scalar_tensor_tensor(out=tiles_of[:, :], in0=tiles_of[:, :], scalar=float(P),
                                                  in1=p_small[:, 32:32 + NT], op0=ALU.mult, op1=ALU.add))
                        go(v.tensor_tensor(pad_ok[:, :], pad_f[:, 0:NT], tiles_of[:, :], ALU.is_ge))
                        go(v.scalar_tensor_tensor(out=pad_f[:, 0:NT], in0=pad_f[:, 0:NT], scalar=float(-ET * P),
                                                  in1=pad_ok[:, :], op0=ALU.add, op1=ALU.mult))
                        go(v.tensor_scalar(pad_f[:, 0:NT], pad_f[:, 0:NT], float(ET * P), None, ALU.add))
                        go(v.tensor_scalar(pad_f[:, NT:2 * NT], iota_f[:, 0:NT], tiles_end[:, NT - 1:NT], float(P),
                                           ALU.add, ALU.mult))
                        go(v.tensor_scalar(pad_f[:, NT:2 * NT], pad_f[:, NT:2 * NT], iota_p[:, :], None, ALU.add))
                        v.tensor_copy(pads[:, :], pad_f[:, :]).then_inc(s_pads, 1)
                        for i in range(4):
                            dve.wait_ge(s_m, i + 1)
                            v.tensor_copy(meta[:, i * q:(i + 1) * q, :].rearrange("p j f -> p f j"), p_meta[i % 2][:, :, 0:q]
                                          ).then_inc(s_mc, 1)
                        dve.wait_ge(s_mc, 4)
                        go(v.tensor_copy(rel_idx[:, :], meta[:, :, 0]))
                        go(v.tensor_scalar(srce[:, :], meta[:, :, 0], 1.0 / H, -(H - 1) / 2 / H, ALU.mult, ALU.add))
                        go(v.tensor_scalar(srce[:, :], srce[:, :], MAGIC, -MAGIC, ALU.add, ALU.add))
                        go(v.tensor_copy(src_idx[:, 0:ET], srce[:, :]))
                        go(v.memset(src_idx[:, ET:ET + T], 0))
                        go(v.scalar_tensor_tensor(out=ldst[:, :], in0=own_rep[:, :], scalar=float(-NP), in1=meta[:, :, 1],
                                                  op0=ALU.mult, op1=ALU.add))
                        go(v.tensor_scalar(owned[:, :], ldst[:, :], 0.0, None, ALU.is_ge))
                        go(v.scalar_tensor_tensor(out=owned[:, :], in0=ldst[:, :], scalar=float(NP), in1=owned[:, :],
                                                  op0=ALU.is_lt, op1=ALU.mult))
                        go(v.scalar_tensor_tensor(out=dst_of[:, :], in0=meta[:, :, 1], scalar=1.0, in1=owned[:, :],
                                                  op0=ALU.add, op1=ALU.mult))
                        v.tensor_scalar(dst_of[:, :], dst_of[:, :], -1.0, None, ALU.add).then_inc(s_ready, 1)
                        dve.wait_ge(s_ready, 1)
                        go(v.tensor_scalar(work[:, :], srce[:, :], 1.0 / NP, -(NP // 2) / NP, ALU.mult, ALU.add))
                        go(v.tensor_scalar(work[:, :], work[:, :], MAGIC, -MAGIC, ALU.add, ALU.add))
                        go(v.scalar_tensor_tensor(out=lsrc[:, :], in0=work[:, :], scalar=float(-NP), in1=srce[:, :],
                                                  op0=ALU.mult, op1=ALU.add))
                        go(v.tensor_scalar(work[:, :], meta[:, :, 3], float(-ET * P), None, ALU.add))
                        go(v.tensor_tensor(work[:, :], work[:, :], owned[:, :], ALU.mult))
                        go(v.tensor_scalar(slot_idx[:, :], work[:, :], float(ET * P), None, ALU.add))
                        for k in range(2):
                            dve.wait_ge(s_tr, k + 1)
                            v.tensor_copy(seqt[:, k, :, :], p_tr[0:q, :, :]).then_inc(s_trc, 1)


        def moments(of, tag):
            with ExitStack() as c:
                st = sb(c, tag + "st", [NP, NTP, 6])
                s_st, s_sq, s_ch = (sem(c, tag + n) for n in ("s_st", "s_sq", "s_ch"))
                with nc.Block() as block:
                    @block.vector
                    def _(dve):
                        v = nc.vector
                        for t in range(NTP):
                            v.bn_stats(st[:, t, :], of[:, t, 0:D]).then_inc(s_st, 1)
                        dve.wait_ge(s_st, NTP)
                        go = Link(dve, s_ch)
                        go(v.tensor_tensor(rstd[:, :], st[:, :, 1], st[:, :, 4], ALU.subtract))
                        go(v.scalar_tensor_tensor(out=rstd[:, :], in0=rstd[:, :], scalar=D / 4, in1=rstd[:, :],
                                                  op0=ALU.mult, op1=ALU.mult))
                        go(v.tensor_tensor(rstd[:, :], rstd[:, :], st[:, :, 2], ALU.add))
                        go(v.tensor_tensor(rstd[:, :], rstd[:, :], st[:, :, 5], ALU.add))
                        go(v.tensor_tensor(nmr[:, :], st[:, :, 1], st[:, :, 4], ALU.add))
                        v.tensor_scalar(rstd[:, :], rstd[:, :], 1.0 / D, EPS, ALU.mult, ALU.add).then_inc(s_sq, 1)
                        dve.wait_ge(s_sq, 2)
                        go(v.reciprocal(rstd[:, :], rstd[:, :]))
                        go(v.scalar_tensor_tensor(out=nmr[:, :], in0=nmr[:, :], scalar=-0.5, in1=rstd[:, :],
                                                  op0=ALU.mult, op1=ALU.mult))

                    @block.scalar
                    def _(act):
                        act.wait_ge(s_sq, 1)
                        nc.scalar.activation(rstd[:, :], rstd[:, :], ACT.Sqrt).then_inc(s_sq, 1)

        def project(tag, w, width, units, put, store=None, copies=2, stores=1, rows=None):
            with ExitStack() as c:
                h = sb(c, tag + "h", [NP, 2, D])
                hT = sb(c, tag + "hT", [P, 2, 2, NP])
                banks = -(-width // 512)
                pT = [ps(c, f"{tag}pT{s}", [P, 2, 256]) for s in range(2)]
                pO = [ps(c, f"{tag}pO{s}", [P, banks * 512]) for s in range(2)]
                s_h, s_t, s_c, s_o, s_e, s_d = ([sem(c, f"{tag}{n}{s}") for s in range(2)]
                                                for n in ("s_h", "s_t", "s_c", "s_o", "s_e", "s_d"))
                U, C = units, copies
                with nc.Block() as block:
                    @block.scalar
                    def _(act):
                        for s in range(2):
                            act.sem_inc(s_e[s], 1)
                        with act.Fori(0, NTP // 2) as it:
                            for s in range(2):
                                t = it * 2 + s
                                act.wait_ge(s_t[s], it + 1)
                                if rows is None:
                                    nc.scalar.activation(h[:, s, :], X[:, bass.ds(t, 1), :].rearrange("p t f -> p (t f)"), ACT.Relu,
                                                         bias=nmr[:, bass.ds(t, 1)], scale=rstd[:, bass.ds(t, 1)]).then_inc(s_h[s], 1)
                                else:
                                    nc.scalar.activation(h[:, s, :], rows[:, bass.ds(t, 1), 0:D].rearrange("p t f -> p (t f)"),
                                                         ACT.Copy).then_inc(s_h[s], 1)
                            put("act", act, it, pO, s_o, s_e, s_d)

                    @block.tensor
                    def _(pe):
                        for s in range(2):
                            pe.sem_inc(s_t[s], 1)
                            pe.sem_inc(s_o[s], 1)
                        with pe.Fori(0, NTP // 2) as it:
                            for s in range(2):
                                pe.wait_ge(s_h[s], it + 1)
                                pe.wait_ge(s_c[s], it + 1)
                                for k in range(2):
                                    ins = nc.tensor.transpose(pT[s][:, k, 0:NP], h[:, s, k * P:(k + 1) * P], ident[0:NP, 0:NP])
                                ins.then_inc(s_t[s], 1)
                            for s in range(2):
                                pe.wait_ge(s_c[s], it + 2)
                                for u in range(U):
                                    z = (s * U + u) % 2
                                    if U == 2:
                                        if s == 0:
                                            pe.wait_ge(s_e[z], it * 2 + 1)
                                        else:
                                            pe.wait_ge(s_e[z], it * 2 + 2)
                                    else:
                                        pe.wait_ge(s_e[z], it * C + 1)
                                    for n0 in range(0, width, 512):
                                        n1 = min(width, n0 + 512)
                                        parts = w(u, n0, n1)
                                        for k, rhs in parts:
                                            ins = nc.tensor.matmul(pO[z][0:NP, n0:n1], hT[:, s, k, :], rhs,
                                                                   start=k == parts[0][0], stop=k == parts[-1][0])
                                    ins.then_inc(s_o[z], 1)

                    @block.vector
                    def _(dve):
                        for s in range(2):
                            dve.sem_inc(s_c[s], 1)
                        with dve.Fori(0, NTP // 2) as it:
                            for s in range(2):
                                dve.wait_ge(s_t[s], it + 2)
                                if U == 2:
                                    dve.wait_ge(s_o[1], it * 2 + 1)
                                else:
                                    dve.wait_ge(s_o[s], it + 1)
                                nc.vector.tensor_copy(hT[:, s, :, :], pT[s][:, :, 0:NP]).then_inc(s_c[s], 1)
                            put("dve", dve, it, pO, s_o, s_e, s_d)

                    if store is not None:
                        @block.sync
                        def _(sp):
                            for s in range(2):
                                sp.sem_inc(s_d[s], 1)
                            with sp.Fori(0, NTP // 2) as it:
                                store(sp, it, s_e, s_d)
                            for s in range(2):
                                sp.wait_ge(s_d[s], stores * 16 * (NTP // 2) + 1)

        def whole(wt):
            return lambda u, n0, n1: [(k, wt[:, k, n0:n1]) for k in range(2)]

        def layer0_in():
            with ExitStack() as c:
                wt = sb(c, "w0", [P, 2, D])
                load_all([(wt[:, :, :], L0_gnn_weight.rearrange("(k p) n -> p k n", p=P))], "w0")
                moments(X, "a0")

                def put(who, eng, it, pO, s_o, s_e, s_d):
                    if who == "act":
                        for s in range(2):
                            eng.wait_ge(s_o[s], it + 2)
                            nc.scalar.activation(table[:, bass.ds(it * 2 + s, 1), :].rearrange("p t f -> p (t f)"),
                                                 pO[s][0:NP, 0:D], ACT.Copy).then_inc(s_e[s], 1)
                project("d0", whole(wt), D, 1, put, copies=1)

        def layer1_in():
            with ExitStack() as c:
                wt = sb(c, "w1", [P, 2, H, P])
                ry = sb(c, "ry", [NP, 2, H, 2, P])
                s_z = sem(c, "w1z")
                with nc.Block() as block:
                    @block.vector
                    def _(dve):
                        nc.vector.memset(wt[:, :, :, :], 0.0).then_inc(s_z, 1)
                        dve.wait_ge(s_z, 1)
                blocks = L1_gnn_weight.rearrange("r (b i o) -> b i r o", b=H, i=DH)
                load_all([(wt[(b % 4) * DH:(b % 4 + 1) * DH, b // 4, :, (b % 4) * DH:(b % 4 + 1) * DH], blocks[b])
                          for b in range(H)], "w1")
                moments(X, "a1")

                def w(u, n0, n1):
                    return [(u, wt[:, u, n0 // P:n1 // P, :])]

                def put(who, eng, it, pO, s_o, s_e, s_d):
                    u = 0 if who == "act" else 1
                    for s in range(2):
                        eng.wait_ge(s_o[u], it * 2 + (s + 2))
                        eng.wait_ge(s_d[s], it * 16 + 1)
                        o = ry[:, s, :, u, :]
                        i = pO[u][0:NP, :].rearrange("p (r f) -> p r f", r=H)
                        if u == 0:
                            nc.scalar.activation(o, i, ACT.Copy).then_inc(s_e[u], 1)
                        else:
                            nc.vector.tensor_copy(o, i).then_inc(s_e[u], 1)

                def store(sp, it, s_e, s_d):
                    for s in range(2):
                        for u in range(2):
                            sp.wait_ge(s_e[u], it * 2 + (s + 2))
                        sp.dma_start(rel_table[bass.ds((it * 2 + s) * (NP * H), NP * H), :].rearrange("(p r) f -> p (r f)", r=H),
                                     ry[:, s, :, :, :].rearrange("p r k f -> p (r k f)")).then_inc(s_d[s], 16)
                project("d1", w, H * P, 2, put, store)

        def layer2_in():
            with ExitStack() as c:
                wt = sb(c, "w2", [P, 2, 3 * D])
                kv = sb(c, "kv", [NP, 2, 2 * D])
                load_all([(wt[:, :, i * D:(i + 1) * D], a.rearrange("(k p) n -> p k n", p=P))
                          for i, a in enumerate((L2_gnn_Wk, L2_gnn_Wv, L2_gnn_Wq))], "w2")
                moments(X, "a2")

                def put(who, eng, it, pO, s_o, s_e, s_d):
                    for s in range(2):
                        eng.wait_ge(s_o[s], it + 2)
                        if who == "act":
                            eng.wait_ge(s_d[s], it * 32 + 1)
                            nc.scalar.activation(kv[:, s, :], pO[s][0:NP, 0:2 * D], ACT.Copy).then_inc(s_e[s], 1)
                        else:
                            nc.vector.tensor_copy(table[:, bass.ds(it * 2 + s, 1), :].rearrange("p t f -> p (t f)"),
                                                  pO[s][0:NP, 2 * D:3 * D]).then_inc(s_e[s], 1)

                def store(sp, it, s_e, s_d):
                    for s in range(2):
                        sp.wait_ge(s_e[s], it * 2 + 3)
                        rows = bass.ds((it * 2 + s) * NP, NP)
                        sp.dma_start(key_table[rows, :], kv[:, s, 0:D]).then_inc(s_d[s], 16)
                        sp.dma_start(value_table[rows, :], kv[:, s, D:2 * D]).then_inc(s_d[s], 16)
                project("d2", whole(wt), 3 * D, 1, put, store, stores=2)

        def layer3_in():
            with ExitStack() as c:
                wt = sb(c, "w3", [P, 2, D + 2 * H])
                av = sb(c, "av", [P, H, 2 * DH])
                wa = sb(c, "wa", [P, H, DH])
                wh = sb(c, "wh", [NP, 2, MW])
                s_ch = sem(c, "w3ch")
                load_all([(wt[:, k, 0:D].rearrange("p (h d) -> p h d", h=H),
                           L3_gnn_W[:, k * P:(k + 1) * P, :].rearrange("h p d -> p h d")) for k in range(2)]
                         + [(av[:, :, :], L3_gnn_a.partition_broadcast(P))], "w3")
                with nc.Block() as block:
                    @block.vector
                    def _(dve):
                        go = Link(dve, s_ch)
                        for k in range(2):
                            for i in range(2):
                                go(nc.vector.tensor_tensor(wa[:, :, :], wt[:, k, 0:D].rearrange("p (h d) -> p h d", h=H),
                                                           av[:, :, i * DH:(i + 1) * DH], ALU.mult))
                                go(nc.vector.tensor_reduce(wt[:, k, D + i * H:D + (i + 1) * H], wa[:, :, :], AX.X, ALU.add))
                moments(X, "a3")

                def put(who, eng, it, pO, s_o, s_e, s_d):
                    if who == "act":
                        for s in range(2):
                            eng.wait_ge(s_o[s], it + 2)
                            eng.wait_ge(s_d[s], it * 32 + 1)
                            nc.scalar.activation(wh[:, s, :], pO[s][0:NP, 0:MW], ACT.Copy).then_inc(s_e[s], 1)
                            nc.scalar.activation(table[:, bass.ds(it * 2 + s, 1), 0:H].rearrange("p t f -> p (t f)"),
                                                 pO[s][0:NP, MW:MW + H], ACT.Copy).then_inc(s_e[s], 1)

                def store(sp, it, s_e, s_d):
                    for s in range(2):
                        sp.wait_ge(s_e[s], it * 2 + 3)
                        rows = bass.ds((it * 2 + s) * NP, NP)
                        sp.dma_start(wh_table[rows, :], wh[:, s, 0:D]).then_inc(s_d[s], 16)
                        sp.dma_start(s1_table[rows, :], wh[:, s, D:MW]).then_inc(s_d[s], 16)
                project("d3", whole(wt), D + 2 * H, 1, put, store, stores=2)

        def load_all(pairs, tag):
            with ExitStack() as c:
                s_l = sem(c, tag + "ld")
                with nc.Block() as block:
                    @block.sync
                    def _(sp):
                        for to, of in pairs:
                            sp.dma_start(to, of).then_inc(s_l, 16)
                        sp.wait_ge(s_l, 16 * len(pairs))

        def add_sums(tag):
            with ExitStack() as c:
                s_a = sem(c, tag + "a")
                with nc.Block() as block:
                    @block.vector
                    def _(dve):
                        nc.vector.tensor_tensor(X[:, 0:NT, :], X[:, 0:NT, :], acc[:, 0:NT, 0:D], ALU.add).then_inc(s_a, 1)
                        dve.wait_ge(s_a, 1)
                        nc.vector.memset(acc[:, :, :], 0.0).then_inc(s_a, 1)

        regs = {e.engine: [e.alloc_register(f"own_{k}_{i}") for i in range(G)]
                for k, e in (("pe", nc.tensor), ("dve", nc.vector))}

        def owners(eng, own, it, q, hi):
            eng.reg_load(regs[eng.engine], own[0:1, bass.ds(it * T + q * G, G)])
            return [eng.snap(r, min_val=0, max_val=hi) for r in regs[eng.engine]]

        def scatter_by_source():
            with ExitStack() as c:
                bl = sb(c, "bl", [NP, NG, G * P])
                oht = sb(c, "oht", [NP, NG, G * P])
                msg = sb(c, "msg", [P, NG, G, MW])
                idx = sb(c, "idx", [P, NG, G], I32)
                dummy = sb(c, "sc_dummy", [1, 1], I32)
                counted = sb(c, "sc_counted", [1, NG])
                pE = [ps(c, f"pE{s}", [P, 512]) for s in range(2)]
                bl_in, scattered = ([sem(c, f"sc_{n}{q}") for q in range(NG)] for n in ("bl_in", "scattered"))
                oht_made, idx_made, expanded, messaged, s_d = (
                    sem(c, "sc_" + n) for n in "oht_made idx_made expanded messaged s_d".split())
                with nc.Block() as block:
                    @block.sync
                    def _(sp):
                        with sp.Fori(0, ITER) as it:
                            for q in range(NG):
                                sp.wait_ge(oht_made, it * NG + (q + 1))
                                sp.dma_start(bl[:, q, :], ldst_seq[bass.ds((it * NG + q) * (G * P), G * P)]
                                             .partition_broadcast(NP)).then_inc(bl_in[q], 16)

                    @block.vector
                    def _(dve):
                        v = nc.vector
                        dve.sem_inc(oht_made, NG)
                        with dve.Fori(0, ITER) as it:
                            for q in range(NG):
                                dve.wait_ge(bl_in[q], it * 16 + 16)
                                dve.wait_ge(expanded, it * T + (q + 1) * G)
                                v.tensor_scalar(oht[:, q, :], bl[:, q, :], iota_p[0:NP, :], None,
                                                ALU.is_equal).then_inc(oht_made, 1)
                                dve.wait_ge(scattered[q], it * (16 * G) + 16)
                                j = bass.ds((it * NG + q) * G, G)
                                v.tensor_copy(msg[:, q, :, D:D + 1], lsrc[:, j].unsqueeze(2)).then_inc(idx_made, 1)
                                v.tensor_copy(idx[:, q, :], slot_idx[:, j]).then_inc(idx_made, 1)

                    @block.tensor
                    def _(pe):
                        pe.sem_inc(expanded, T)
                        with pe.Fori(0, ITER) as it:
                            for q in range(NG):
                                own = owners(pe, own_d, it, q, NT)
                                pe.wait_ge(oht_made, it * NG + (NG + q + 1))
                                for i in range(G):
                                    n = q * G + i
                                    pe.wait_ge(messaged, it * T + (T + n - 1))
                                    nc.tensor.matmul(pE[n % 2][:, 0:D], oht[:, q, i * P:(i + 1) * P],
                                                     table[:, bass.ds(own[i], 1), :], start=True, stop=True
                                                     ).then_inc(expanded, 1)

                    @block.scalar
                    def _(act):
                        act.sem_inc(messaged, T)
                        with act.Fori(0, ITER) as it:
                            for q in range(NG):
                                act.wait_ge(scattered[q], it * (16 * G) + 16)
                                for i in range(G):
                                    n = q * G + i
                                    act.wait_ge(expanded, it * T + (T + n + 1))
                                    nc.scalar.activation(msg[:, q, i, 0:D], pE[n % 2][:, 0:D], ACT.Copy,
                                                         scale=meta[:, bass.ds(it * T + n, 1), 2]).then_inc(messaged, 1)

                    @block.gpsimd
                    def _(pool):
                        nc.gpsimd.memset(dummy[:, :], 0).then_inc(s_d, 1)
                        nc.gpsimd.memset(msg[:, :, :, D + 1:MW], 0.0).then_inc(s_d, 1)
                        pool.wait_ge(s_d, 2)
                        for q in range(NG):
                            nc.gpsimd.dma_start(counted[:, q:q + 1], iota_f[0:1, q:q + 1]).then_inc(scattered[q], 16)
                        with pool.Fori(0, ITER) as it:
                            for q in range(NG):
                                pool.wait_ge(idx_made, it * (2 * NG) + 2 * (q + 1))
                                pool.wait_ge(messaged, it * T + (T + (q + 1) * G))
                                pool.wait_ge(s_d, it * NG + (q + 2))
                                nc.gpsimd.tensor_tensor(dummy[:, :], dummy[:, :], dummy[:, :], ALU.add).then_inc(s_d, 1)
                                for i in range(G):
                                    nc.gpsimd.indirect_dma_start(
                                        by_src, bass.IndirectOffsetOnAxis(ap=idx[:, q, i:i + 1], axis=0), msg[:, q, i, :], None,
                                        bounds_check=ET * P - 1, oob_is_err=False).then_inc(scattered[q], 16)
                        for q in range(NG):
                            pool.wait_ge(scattered[q], ITER * 16 * G + 16)

        def sum_over_edges(tag, own, gather=None, weighted=False, probs=False):
            width = MW if probs else D
            with ExitStack() as c:
                msg = sb(c, tag + "msg", [P, NG, G, MW])
                oh = sb(c, tag + "oh", [P, T, NP])
                idx = sb(c, tag + "idx", [P, NG, G], I32)
                prows = sb(c, tag + "prows", [10 * H, 2, P])
                pcols = sb(c, tag + "pcols", [P, T, H])
                dummy = sb(c, tag + "dummy", [1, 1], I32)
                pM = [ps(c, f"{tag}pM{i}", [P, 512]) for i in range(G)]
                pT = [ps(c, f"{tag}pT{i}", [P, 512]) for i in range(2)]
                filled = [sem(c, f"{tag}filled{q}") for q in range(NG)]
                p_in = [sem(c, f"{tag}p_in{k}") for k in range(2)]
                idx_made, oh_made, summed, added, turned, copied, prepared, s_d = (
                    sem(c, tag + n) for n in "idx_made oh_made summed added turned copied prepared s_d".split())
                table_of, index = gather or (None, None)
                fill = 16 * (G if gather else 1)
                with nc.Block() as block:
                    @block.sync
                    def _(sp):
                        if probs or not gather:
                            with sp.Fori(0, ITER) as it:
                                if probs:
                                    for k in range(2):
                                        sp.wait_ge(turned, it * 2 + 1)
                                        sp.dma_start(prows[:, k, :], prob_rows[bass.ds((it * T + k * 10) * H, 10 * H), :]
                                                     ).then_inc(p_in[k], 16)
                                if not gather:
                                    for q in range(NG):
                                        sp.wait_ge(summed, it * T + (q + 1) * G)
                                        sp.dma_start(msg[:, q, :, :], by_src[bass.ds((it * T + q * G) * P, G * P), :]
                                                     .rearrange("(t p) f -> p t f", p=P)).then_inc(filled[q], 16)

                    @block.gpsimd
                    def _(pool):
                        if gather:
                            nc.gpsimd.memset(dummy[:, :], 0).then_inc(s_d, 1)
                            with pool.Fori(0, ITER) as it:
                                for q in range(NG):
                                    pool.wait_ge(idx_made, it * NG + (q + 1))
                                    pool.wait_ge(summed, it * T + (q + 1) * G)
                                    pool.wait_ge(s_d, it * NG + (q + 1))
                                    nc.gpsimd.tensor_tensor(dummy[:, :], dummy[:, :], dummy[:, :], ALU.add).then_inc(s_d, 1)
                                    for i in range(G):
                                        nc.gpsimd.indirect_dma_start(
                                            msg[:, q, i, 0:D], None, table_of,
                                            bass.IndirectOffsetOnAxis(ap=idx[:, q, i:i + 1], axis=0)).then_inc(filled[q], 16)

                    @block.scalar
                    def _(act):
                        act.sem_inc(copied, 1)
                        if gather:
                            with act.Fori(0, ITER) as it:
                                for q in range(NG):
                                    act.wait_ge(summed, it * T + (q + 1) * G)
                                    nc.scalar.activation(idx[:, q, :], index[:, bass.ds((it * NG + q) * G, G)],
                                                         ACT.Copy).then_inc(idx_made, 1)
                                if probs:
                                    for k in range(2):
                                        act.wait_ge(turned, it * 2 + (k + 2))
                                        act.wait_ge(prepared, it * NG + 1)
                                        nc.scalar.activation(pcols[:, k * 10:(k + 1) * 10, :].rearrange("p t h -> p (t h)"),
                                                             pT[k][:, 0:10 * H], ACT.Copy).then_inc(copied, 1)

                    @block.tensor
                    def _(pe):
                        pe.sem_inc(turned, 1)
                        pe.sem_inc(summed, T)
                        with pe.Fori(0, ITER) as it:
                            if probs:
                                pe.wait_ge(copied, it * 2 + 1)
                                for k in range(2):
                                    pe.wait_ge(p_in[k], it * 16 + 16)
                                    nc.tensor.transpose(pT[k][:, 0:10 * H], prows[:, k, :], ident[0:10 * H, 0:10 * H]
                                                        ).then_inc(turned, 1)
                            for q in range(NG):
                                pe.wait_ge(filled[q], it * fill + fill)
                                pe.wait_ge(oh_made, it * NG + (q + 1))
                                for i in range(G):
                                    n = q * G + i
                                    pe.wait_ge(added, it * T + (n + 1))
                                    nc.tensor.matmul(pM[i][0:NP, 0:width], oh[:, n, :], msg[:, q, i, 0:width],
                                                     start=True, stop=True).then_inc(summed, 1)

                    @block.vector
                    def _(dve):
                        v = nc.vector

                        def add(it, q):
                            node_tile = owners(dve, own, it, q, NT)
                            for i in range(G):
                                n = q * G + i
                                dve.wait_ge(summed, it * T + (T + n + 1))
                                dve.wait_ge(added, it * T + (n + G))
                                at = acc[:, bass.ds(node_tile[i], 1), 0:width]
                                v.tensor_tensor(at, at, pM[i][0:NP, 0:width].unsqueeze(1), ALU.add).then_inc(added, 1)

                        dve.sem_inc(added, G)
                        dve.sem_inc(prepared, 1)
                        with dve.Fori(0, ITER) as it:
                            for q in range(NG):
                                at = bass.ds((it * NG + q) * G, G)
                                if probs:
                                    dve.wait_ge(filled[q], it * fill + fill)
                                    dve.wait_ge(copied, it * 2 + (q // 2 + 2))
                                    m = msg[:, q, :, 0:D].rearrange("p g (h d) -> p g h d", h=H)
                                    pq = pcols[:, q * G:(q + 1) * G, :]
                                    v.tensor_tensor(m, m, pq.unsqueeze(3).to_broadcast([P, G, H, DH]), ALU.mult)
                                    v.tensor_copy(msg[:, q, :, D:MW], pq).then_inc(prepared, 1)
                                    place = ldst[:, at].unsqueeze(2)
                                elif gather:
                                    place = ldst[:, at].unsqueeze(2)
                                else:
                                    dve.wait_ge(filled[q], it * fill + fill)
                                    place = msg[:, q, :, D:D + 1]
                                o = oh[:, q * G:(q + 1) * G, :]
                                if weighted:
                                    for i in range(G):
                                        j = bass.ds(it * T + (q * G + i), 1)
                                        ins = v.tensor_scalar(oh[:, q * G + i, :], iota_f[:, 0:NP], ldst[:, j], meta[:, j, 2],
                                                              ALU.is_equal, ALU.mult)
                                else:
                                    ins = v.tensor_tensor(o, iota_f[:, 0:NP].unsqueeze(1).to_broadcast([P, G, NP]),
                                                          place.to_broadcast([P, G, NP]), ALU.is_equal)
                                ins.then_inc(oh_made, 1)
                                if q:
                                    add(it, q - 1)
                            add(it, NG - 1)

        def scores(tag, table_of, width):
            dots = width == D
            with ExitStack() as c:
                bl = sb(c, tag + "bl", [NP, NG, G * P])
                oht = sb(c, tag + "oht", [NP, NG, G * P])
                rows = sb(c, tag + "rows", [P, NG, G, width])
                prod = sb(c, tag + "prod", [P, 2, G, width])
                idx = sb(c, tag + "idx", [P, NG, G], I32)
                sc = sb(c, tag + "sc", [P, T, H])
                srow = sb(c, tag + "srow", [10 * H, 2, P])
                dummy = sb(c, tag + "dummy", [1, 1], I32)
                pE = [ps(c, f"{tag}pE{s}", [P, 6 * 256]) for s in range(2)]
                pT = [ps(c, f"{tag}pT{s}", [P, 512]) for s in range(2)]
                bl_in, gathered = ([sem(c, f"{tag}{n}{q}") for q in range(NG)] for n in ("bl_in", "gathered"))
                stored = [sem(c, f"{tag}stored{k}") for k in range(2)]
                oht_made, idx_made, expanded, scored, multiplied, turned, copied, s_d = (
                    sem(c, tag + n) for n in "oht_made idx_made expanded scored multiplied turned copied s_d".split())
                with nc.Block() as block:
                    @block.sync
                    def _(sp):
                        with sp.Fori(0, ITER) as it:
                            for q in range(NG):
                                sp.wait_ge(oht_made, it * NG + (q + 1))
                                sp.dma_start(bl[:, q, :], ldst_seq[bass.ds((it * NG + q) * (G * P), G * P)]
                                             .partition_broadcast(NP)).then_inc(bl_in[q], 16)

                    @block.gpsimd
                    def _(pool):
                        nc.gpsimd.memset(dummy[:, :], 0).then_inc(s_d, 1)
                        with pool.Fori(0, ITER) as it:
                            for q in range(NG):
                                pool.wait_ge(idx_made, it * NG + (q + 1))
                                pool.wait_ge(multiplied, it * NG + (q + 1))
                                pool.wait_ge(s_d, it * NG + (q + 1))
                                nc.gpsimd.tensor_tensor(dummy[:, :], dummy[:, :], dummy[:, :], ALU.add).then_inc(s_d, 1)
                                for i in range(G):
                                    nc.gpsimd.indirect_dma_start(
                                        rows[:, q, i, :], None, table_of,
                                        bass.IndirectOffsetOnAxis(ap=idx[:, q, i:i + 1], axis=0)).then_inc(gathered[q], 16)

                    @block.tensor
                    def _(pe):
                        pe.sem_inc(turned, 1)
                        pe.sem_inc(expanded, NG)

                        def turn(it, k):
                            pe.wait_ge(scored, it * NG + (2 * k + 3))
                            pe.wait_ge(copied, it * 2 + (k + 1))
                            nc.tensor.transpose(pT[k][0:10 * H, 0:P], sc[:, k * 10:(k + 1) * 10, :].rearrange("p t h -> p (t h)"),
                                                ident[:, :]).then_inc(turned, 1)

                        with pe.Fori(0, ITER) as it:
                            for q in range(NG):
                                own = owners(pe, own_d, it, q, NT)
                                pe.wait_ge(oht_made, it * NG + (NG + q + 1))
                                pe.wait_ge(multiplied, it * NG + (NG + q - 1))
                                for i in range(G):
                                    ins = nc.tensor.matmul(pE[q % 2][:, i * width:(i + 1) * width], oht[:, q, i * P:(i + 1) * P],
                                                           table[:, bass.ds(own[i], 1), 0:width], start=True, stop=True)
                                ins.then_inc(expanded, 1)
                                if q == 2:
                                    turn(it, 0)
                            turn(it, 1)

                    @block.scalar
                    def _(act):
                        act.sem_inc(copied, 1)
                        for k in range(2):
                            act.sem_inc(stored[k], 1)
                        with act.Fori(0, ITER) as it:
                            for k in range(2):
                                act.wait_ge(turned, it * 2 + (k + 2))
                                act.wait_ge(stored[k], it * 16 + 1)
                                nc.scalar.activation(srow[:, k, :], pT[k][0:10 * H, 0:P], ACT.Copy).then_inc(copied, 1)
                                act.wait_ge(copied, it * 2 + (k + 2))
                                act.dma_start(score_rows[bass.ds((it * T + k * 10) * H, 10 * H), :], srow[:, k, :]
                                              ).then_inc(stored[k], 16)
                        for k in range(2):
                            act.wait_ge(stored[k], ITER * 16 + 1)

                    @block.vector
                    def _(dve):
                        v = nc.vector
                        dve.sem_inc(oht_made, NG)
                        dve.sem_inc(multiplied, NG)
                        dve.sem_inc(scored, 1)
                        for q in range(NG):
                            v.tensor_copy(idx[:, q, :], src_idx[:, q * G:(q + 1) * G]).then_inc(idx_made, 1)

                        def head_sums(it, q):
                            dve.wait_ge(multiplied, it * NG + (NG + q + 1))
                            v.tensor_reduce(sc[:, q * G:(q + 1) * G, :], prod[:, q % 2, :, :].rearrange("p g (h d) -> p g h d", h=H),
                                            AX.X, ALU.add).then_inc(scored, 1)

                        with dve.Fori(0, ITER) as it:
                            for q in range(NG):
                                dve.wait_ge(bl_in[q], it * 16 + 16)
                                dve.wait_ge(expanded, it * NG + (q + 1))
                                v.tensor_scalar(oht[:, q, :], bl[:, q, :], iota_p[0:NP, :], None,
                                                ALU.is_equal).then_inc(oht_made, 1)
                            for q in range(NG):
                                if q == 0:
                                    dve.wait_ge(turned, it * 2 + 1)
                                if dots and q:
                                    head_sums(it, q - 1)
                                dve.wait_ge(gathered[q], it * (16 * G) + 16 * G)
                                dve.wait_ge(expanded, it * NG + (NG + q + 1))
                                e = pE[q % 2][:, 0:G * width].rearrange("p (g f) -> p g f", g=G)
                                v.tensor_copy(idx[:, q, :], src_idx[:, bass.ds(it * T + (T + q * G), G)]).then_inc(idx_made, 1)
                                if dots:
                                    dve.wait_ge(scored, it * NG + (q or 1))
                                    v.tensor_tensor(prod[:, q % 2, :, :], rows[:, q, :, :], e, ALU.mult).then_inc(multiplied, 1)
                                else:
                                    v.tensor_tensor(sc[:, q * G:(q + 1) * G, :], rows[:, q, :, :], e, ALU.add
                                                    ).then_inc(multiplied, 1)
                                    dve.wait_ge(multiplied, it * NG + (NG + q + 1))
                                    dve.sem_inc(scored, 1)
                            if dots:
                                head_sums(it, NG - 1)

        def softmax(tag, floor_zero, slope, scale):
            with ExitStack() as c:
                s, m = sb(c, tag + "s", [P, CE]), sb(c, tag + "m", [P, CE])
                seq = sb(c, tag + "seq", [P, CE + 2])
                mask = sb(c, tag + "mask", [P, CE])
                ends = sb(c, tag + "ends", [P, 4])
                row = sb(c, tag + "row", [1, 4, P])
                enter = sb(c, tag + "enter", [P, 2])
                pR = ps(c, tag + "pR", [P, 512])
                pC = ps(c, tag + "pC", [P, 512])
                s_in, s_pe, s_ch, s_e, s_p, s_out = (sem(c, tag + n) for n in "s_in s_pe s_ch s_e s_p s_out".split())
                by_head = score_rows.rearrange("(c t h) p -> h c t p", c=CH, t=CT, h=H)
                to_head = prob_rows.rearrange("(c t h) p -> h c t p", c=CH, t=CT, h=H)
                with nc.Block() as block:
                    @block.sync
                    def _(sp):
                        for h in range(H):
                            rows = slice(h * CH, (h + 1) * CH)
                            sp.dma_start(s[rows, :].rearrange("c (t p) -> c t p", p=P), by_head[h]).then_inc(s_in, 16)
                            for a, b in ((0, CE), (CE, CE + 2)):
                                at = dst_seq[P - 1 + a:P - 1 + a + SQ * P].rearrange("(c e) -> c e", c=CH)
                                sp.dma_start(seq[rows, a:b], at[:, 0:b - a]).then_inc(s_in, 16)
                        sp.wait_ge(s_p, 1)
                        for h in range(H):
                            sp.dma_start(to_head[h], s[h * CH:(h + 1) * CH, :].rearrange("c (t p) -> c t p", p=P)
                                         ).then_inc(s_out, 16)
                        sp.wait_ge(s_out, 16 * H)

                    @block.tensor
                    def _(pe):
                        for d in range(2):
                            pe.wait_ge(s_e, 2 * d + 1)
                            for k in range(2):
                                ins = nc.tensor.transpose(pR[0:1, k * P:(k + 1) * P], ends[:, 2 * d + k:2 * d + k + 1], ident[:, :])
                            ins.then_inc(s_pe, 1)
                            pe.wait_ge(s_e, 2 * d + 2)
                            nc.tensor.transpose(pC[:, d:d + 1], row[:, 3, :], ident[0:1, 0:1]).then_inc(s_pe, 1)

                    @block.vector
                    def _(dve):
                        v = nc.vector
                        go = Link(dve, s_ch)
                        dve.wait_ge(s_in, 16 * 3 * H)
                        if floor_zero:
                            go(v.tensor_scalar(s[:, :], s[:, :], scale, None, ALU.mult))
                        else:
                            go(v.scalar_tensor_tensor(out=s[:, :], in0=s[:, :], scalar=slope, in1=s[:, :],
                                                      op0=ALU.mult, op1=ALU.max))
                        for d in range(2):
                            go(v.tensor_tensor(mask[:, :], seq[:, 1:CE + 1], seq[:, 2 * d:CE + 2 * d], ALU.not_equal))
                            go(v.tensor_scalar(mask[:, :], mask[:, :], -BIG, None, ALU.mult))
                            back = (lambda a: a[:, ::-1]) if d else (lambda a: a[:, :])
                            of = m if d else s
                            end = 0 if d else CE - 1
                            go(v.tensor_tensor_scan(back(m), back(mask), back(of), -BIG, ALU.add, ALU.max))
                            go(v.tensor_copy(ends[:, 2 * d:2 * d + 1], m[:, end:end + 1]))
                            v.tensor_reduce(ends[:, 2 * d + 1:2 * d + 2], mask[:, :], AX.X, ALU.min).then_inc(s_e, 1)
                            dve.wait_ge(s_pe, 2 * d + 1)
                            go(v.tensor_copy(row[:, 0, :], pR[0:1, 0:P]))
                            go(v.tensor_copy(row[:, 1, :], pR[0:1, P:2 * P]))
                            turn = (lambda a: a[:, ::-1]) if d else (lambda a: a)
                            go(v.tensor_tensor_scan(turn(row[:, 2, :]), turn(row[:, 1, :]), turn(row[:, 0, :]), -BIG,
                                                    ALU.add, ALU.max))
                            go(v.memset(row[:, 3, :], -BIG))
                            if d:
                                go(v.tensor_copy(row[:, 3, 0:P - 1], row[:, 2, 1:P]))
                            else:
                                go(v.tensor_copy(row[:, 3, 1:P], row[:, 2, 0:P - 1]))
                            v.memset(row[:, 0, :], 0.0).then_inc(s_e, 1)
                            dve.wait_ge(s_pe, 2 * d + 2)
                            go(v.tensor_copy(enter[:, d:d + 1], pC[:, d:d + 1]))
                            if d:
                                go(v.tensor_tensor_scan(back(m), back(mask), back(m), enter[:, d:d + 1], ALU.add, ALU.max))
                            else:
                                go(v.tensor_tensor_scan(m[:, :], mask[:, :], s[:, :], enter[:, d:d + 1], ALU.add, ALU.max))
                        if floor_zero:
                            go(v.tensor_scalar(m[:, :], m[:, :], 0.0, None, ALU.max))
                        v.tensor_tensor(s[:, :], s[:, :], m[:, :], ALU.subtract).then_inc(s_e, 1)

                    @block.scalar
                    def _(act):
                        act.wait_ge(s_e, 5)
                        nc.scalar.activation(s[:, :], s[:, :], ACT.Exp).then_inc(s_p, 1)

        def divide(tag, add, least):
            with ExitStack() as c:
                s_ch = sem(c, tag + "ch")
                with nc.Block() as block:
                    @block.vector
                    def _(dve):
                        v, go = nc.vector, Link(dve, s_ch)
                        den = acc[:, :, D:MW]
                        go(v.tensor_scalar(den, den, add, least, ALU.add, ALU.max))
                        go(v.reciprocal(den, den))
                        for h in range(H):
                            a = acc[:, :, h * DH:(h + 1) * DH]
                            v.tensor_tensor(a, a, acc[:, :, D + h:D + h + 1].to_broadcast([NP, NTP, DH]), ALU.mult).then_inc(s_ch, 1)
                        dve.wait_ge(s_ch, 2 + H)

        def normalise(tag, to, of, func, gain=None, shift=None):
            with ExitStack() as c:
                s_n, s_ch = sem(c, tag + "n"), sem(c, tag + "ch")
                with nc.Block() as block:
                    @block.scalar
                    def _(act):
                        with act.Fori(0, NTP) as t:
                            flat = lambda a: a[:, bass.ds(t, 1), 0:D].rearrange("p t f -> p (t f)")
                            nc.scalar.activation(flat(to), flat(of), func, bias=nmr[:, bass.ds(t, 1)],
                                                 scale=rstd[:, bass.ds(t, 1)]).then_inc(s_n, 1)

                    if gain is not None:
                        @block.vector
                        def _(dve):
                            go = Link(dve, s_ch)
                            dve.wait_ge(s_n, NTP)
                            wide = [NP, NTP, D]
                            go(nc.vector.tensor_tensor(to[:, :, :], to[:, :, :], gain[0:NP, :].unsqueeze(1).to_broadcast(wide), ALU.mult))
                            go(nc.vector.tensor_tensor(to[:, :, :], to[:, :, :], shift[0:NP, :].unsqueeze(1).to_broadcast(wide), ALU.add))

        def add_row(tag, to, row):
            with ExitStack() as c:
                s_ch = sem(c, tag + "ch")
                with nc.Block() as block:
                    @block.vector
                    def _(dve):
                        nc.vector.tensor_tensor(to[:, :, :], to[:, :, :], row[0:NP, :].unsqueeze(1).to_broadcast([NP, NTP, D]),
                                                ALU.add).then_inc(s_ch, 1)
                        dve.wait_ge(s_ch, 1)

        def feed_forward(w1, w2, b1):
            F = 4
            with ExitStack() as c:
                uT = sb(c, "uT", [P, 2, 2, NP])
                gT = sb(c, "gT", [P, 2, F, NP])
                u = sb(c, "u", [NP, 2, D])
                pT = [ps(c, f"ffT{s}", [P, 2, 256]) for s in range(2)]
                pH = [ps(c, f"ffH{s}", [P, F, P]) for s in range(2)]
                pO = [ps(c, f"ffO{s}", [P, 512]) for s in range(2)]
                s_u, s_t, s_c, s_h, s_g, s_o, s_a = ([sem(c, f"ff_{n}{s}") for s in range(2)]
                                                     for n in "u t c h g o a".split())
                with nc.Block() as block:
                    @block.tensor
                    def _(pe):
                        for s in range(2):
                            for counted in (s_t[s], s_h[s], s_o[s]):
                                pe.sem_inc(counted, 1)
                        with pe.Fori(0, NTP // 2) as it:
                            for s in range(2):
                                pe.wait_ge(s_u[s], it + 1)
                                pe.wait_ge(s_c[s], it + 1)
                                for k in range(2):
                                    ins = nc.tensor.transpose(pT[s][:, k, 0:NP], u[:, s, k * P:(k + 1) * P], ident[0:NP, 0:NP])
                                ins.then_inc(s_t[s], 1)
                            for s in range(2):
                                pe.wait_ge(s_c[s], it + 2)
                                pe.wait_ge(s_g[s], it * F + 1)
                                for f in range(F):
                                    for k in range(2):
                                        ins = nc.tensor.matmul(pH[s][:, f, 0:NP], w1[:, k, f * P:(f + 1) * P], uT[:, s, k, :],
                                                               start=k == 0, stop=k == 1)
                                ins.then_inc(s_h[s], 1)
                            for s in range(2):
                                pe.wait_ge(s_g[s], it * F + (F + 1))
                                pe.wait_ge(s_a[s], it + 1)
                                for f in range(F):
                                    ins = nc.tensor.matmul(pO[s][0:NP, 0:D], gT[:, s, f, :], w2[:, f, :], start=f == 0, stop=f == F - 1)
                                ins.then_inc(s_o[s], 1)

                    @block.scalar
                    def _(act):
                        for s in range(2):
                            act.sem_inc(s_g[s], 1)
                        with act.Fori(0, NTP // 2) as it:
                            for s in range(2):
                                act.wait_ge(s_t[s], it + 1)
                                nc.scalar.activation(u[:, s, :], table[:, bass.ds(it * 2 + s, 1), :].rearrange("p t f -> p (t f)"),
                                                     ACT.Copy).then_inc(s_u[s], 1)
                            for s in range(2):
                                act.wait_ge(s_h[s], it + 2)
                                act.wait_ge(s_o[s], it + 1)
                                for f in range(F):
                                    nc.scalar.activation(gT[:, s, f, :], pH[s][:, f, 0:NP], ACT.Gelu,
                                                         bias=b1[:, f:f + 1]).then_inc(s_g[s], 1)

                    @block.vector
                    def _(dve):
                        for s in range(2):
                            dve.sem_inc(s_c[s], 1)
                            dve.sem_inc(s_a[s], 1)
                        with dve.Fori(0, NTP // 2) as it:
                            for s in range(2):
                                dve.wait_ge(s_t[s], it + 2)
                                dve.wait_ge(s_h[s], it + 1)
                                nc.vector.tensor_copy(uT[:, s, :, :], pT[s][:, :, 0:NP]).then_inc(s_c[s], 1)
                            for s in range(2):
                                dve.wait_ge(s_o[s], it + 2)
                                at = table[:, bass.ds(it * 2 + s, 1), :]
                                nc.vector.tensor_tensor(at, at, pO[s][0:NP, 0:D].unsqueeze(1), ALU.add).then_inc(s_a[s], 1)

        def transformer_rest():
            with ExitStack() as c:
                wo = sb(c, "wo", [P, 2, D])
                vecs = sb(c, "vecs", [P, 6, D])
                w1 = sb(c, "w1f", [P, 2, 2 * D])
                w2 = sb(c, "w2f", [P, 4, D])
                b1 = sb(c, "b1f", [P, 4])
                load_all([(wo[:, :, :], L2_gnn_Wo_w.rearrange("(k p) n -> p k n", p=P)),
                          (w1[:, :, :], L2_gnn_ffn_w1.rearrange("(k p) n -> p k n", p=P)),
                          (w2[:, :, :], L2_gnn_ffn_w2.rearrange("(k p) n -> p k n", p=P)),
                          ] + [(b1[:, f:f + 1], L2_gnn_ffn_b1[f * P:(f + 1) * P].rearrange("(p o) -> p o", o=1)) for f in range(4)]
                         + [(vecs[:, i, :], a.partition_broadcast(P)) for i, a in enumerate(
                             (L2_gnn_Wo_b, L2_gnn_ln1_g, L2_gnn_ln1_b, L2_gnn_ffn_b2, L2_gnn_ln2_g, L2_gnn_ln2_b))], "fw")
                divide("dv2", 1e-8, 0.0)
                normalise("n2", table, X, ACT.Relu)
                add_row("bo", table, vecs[:, 0, :])

                def put(who, eng, it, pO, s_o, s_e, s_d):
                    if who == "dve":
                        for s in range(2):
                            eng.wait_ge(s_o[s], it + 2)
                            at = table[:, bass.ds(it * 2 + s, 1), :]
                            nc.vector.tensor_tensor(at, at, pO[s][0:NP, 0:D].unsqueeze(1), ALU.add).then_inc(s_e[s], 1)
                project("dO", whole(wo), D, 1, put, copies=1, rows=acc)
                moments(table, "m1")
                normalise("n3", table, table, ACT.Identity, vecs[:, 1, :], vecs[:, 2, :])
                feed_forward(w1, w2, b1)
                add_row("b2", table, vecs[:, 3, :])
                moments(table, "m2")
                normalise("n4", table, table, ACT.Identity, vecs[:, 4, :], vecs[:, 5, :])
                s_a = sem(c, "resid")
                with nc.Block() as block:
                    @block.vector
                    def _(dve):
                        nc.vector.tensor_tensor(X[:, :, :], X[:, :, :], table[:, :, :], ALU.add).then_inc(s_a, 1)
                        nc.vector.memset(acc[:, :, :], 0.0).then_inc(s_a, 1)

        def write_out():
            with ExitStack() as c:
                s_o = sem(c, "written")
                with nc.Block() as block:
                    @block.sync
                    def _(sp):
                        sp.dma_start(out.rearrange("(t p) f -> p t f", p=NP), X[:, 0:NT, :]).then_inc(s_o, 16)
                        sp.wait_ge(s_o, 16)

        stages = [constants_and_edges,
                  layer0_in, scatter_by_source,
                  lambda: sum_over_edges("g0", own_s), lambda: add_sums("g0"),
                  layer1_in, lambda: sum_over_edges("g1", own_d, (rel_table, rel_idx), weighted=True), lambda: add_sums("g1"),
                  layer2_in, lambda: scores("c2", key_table, D), lambda: softmax("f2", True, None, SCALE),
                  lambda: sum_over_edges("g2", own_d, (value_table, src_idx), probs=True), transformer_rest,
                  layer3_in, lambda: scores("c3", s1_table, H), lambda: softmax("f3", False, 0.2, None),
                  lambda: sum_over_edges("g3", own_d, (wh_table, src_idx), probs=True),
                  lambda: divide("dv3", 0.0, 1e-30), lambda: add_sums("g3"), write_out]
        for run in stages[:stop_after]:
            run()


_INS = ['x', 'src', 'dst', 'edge_type_8', 'edge_weight', 'L0_gnn_weight', 'L1_gnn_weight', 'L2_gnn_Wq', 'L2_gnn_Wk',
        'L2_gnn_Wv', 'L2_gnn_Wo_w', 'L2_gnn_Wo_b', 'L2_gnn_ln1_g', 'L2_gnn_ln1_b', 'L2_gnn_ln2_g', 'L2_gnn_ln2_b',
        'L2_gnn_ffn_w1', 'L2_gnn_ffn_b1', 'L2_gnn_ffn_w2', 'L2_gnn_ffn_b2', 'L3_gnn_W', 'L3_gnn_a']


def kernel(**inputs):
    import numpy as _np
    import concourse.bacc as _bacc
    from concourse import mybir as _mybir
    from concourse.bass_utils import run_bass_kernel_spmd as _run

    nc = _bacc.Bacc("TRN2", target_bir_lowering=False, num_devices=1)
    arrays, args = {}, []
    for name in _INS:
        a = _np.ascontiguousarray(inputs[name])
        arrays[f"in_{name}"] = a
        args.append(nc.dram_tensor(f"in_{name}", a.shape, _mybir.dt.from_np(a.dtype), kind="ExternalInput").ap())
    args.append(nc.dram_tensor("out_x", (N, D), _mybir.dt.float32, kind="ExternalOutput").ap())
    build(nc, *args)
    r = _run(nc, [arrays], core_ids=[0])
    return r.results[0]["out_x"]
```

```python
from contextlib import ExitStack

import concourse.bass as bass
from concourse import mybir
from concourse.alu_op_type import AluOpType as ALU

ACT = mybir.ActivationFunctionType
AX = mybir.AxisListType
F32 = mybir.dt.float32
I32 = mybir.dt.int32
BF16 = mybir.dt.bfloat16

P = 128
N = 3125
D = 256
E = 53125
H = 8
DH = D // H
NP = 125
NT = N // NP
NTP = NT + 1
EC = -(-E // P)
ET = EC + NT - 1
G = 5
NG = 4
ITER = ET // (G * NG)
CH = 16
CT = -(-ET // CH)
SQ = CH * CT
CE = CT * P
MAGIC = 12582912.0
BIG = 1e30
SCALE = DH ** -0.5
EPS = 1e-5
T = G * NG
MW = D + H
assert ET == ITER * G * NG and N == NT * NP




class Link:

    def __init__(self, eng, sem):
        self.eng, self.sem, self.n = eng, sem, 0

    def __call__(self, ins):
        self.n += 1
        ins.then_inc(self.sem, 1)
        self.eng.wait_ge(self.sem, self.n)


def build(nc, x, src, dst, edge_type_8, edge_weight, L0_gnn_weight, L1_gnn_weight, L2_gnn_Wq, L2_gnn_Wk,
          L2_gnn_Wv, L2_gnn_Wo_w, L2_gnn_Wo_b, L2_gnn_ln1_g, L2_gnn_ln1_b, L2_gnn_ln2_g, L2_gnn_ln2_b,
          L2_gnn_ffn_w1, L2_gnn_ffn_b1, L2_gnn_ffn_w2, L2_gnn_ffn_b2, L3_gnn_W, L3_gnn_a, out):
    top = ExitStack()

    def dram(name, shape):
        return nc.dram_tensor(name, shape, F32, kind="Internal").ap()

    edges = dram("edges", [EC, P * 4])
    ordered = dram("ordered", [EC * P, 4])
    dst_seq = dram("dst_seq", [P + SQ * P + CE])
    ldst_seq = dram("ldst_seq", [ET * P])
    by_src = dram("by_src", [ET * P, MW])
    rel_table = dram("rel_table", [NTP * NP * H, D])
    key_table = dram("key_table", [NTP * NP, D])
    value_table = dram("value_table", [NTP * NP, D])
    wh_table = dram("wh_table", [NTP * NP, D])
    s1_table = dram("s1_table", [NTP * NP, H])
    score_rows = dram("score_rows", [SQ * H, P])
    prob_rows = dram("prob_rows", [SQ * H, P])

    with top:
        def sb(ctx, name, shape, dt=F32):
            return ctx.enter_context(nc.sbuf_tensor(name, shape, dt))

        def ps(ctx, name, shape):
            return ctx.enter_context(nc.psum_tensor(name, shape, F32))

        held = {}

        def sem(ctx, name):
            if ctx not in held:
                held[ctx] = []
                ctx.callback(clear, ctx)
            held[ctx].append(nc.alloc_semaphore(name=name))
            return held[ctx][-1]

        def clear(ctx):
            nc.all_engine_barrier()
            nc.clear_and_free_semaphores(held.pop(ctx))
            nc.all_engine_barrier()

        X = sb(top, "X", [NP, NTP, D])
        acc = sb(top, "acc", [NP, NTP, MW])
        table = sb(top, "table", [NP, NTP, D])
        ident = sb(top, "ident", [P, P])
        iota_f = sb(top, "iota_f", [P, P])
        iota_p = sb(top, "iota_p", [P, 1])
        ones = sb(top, "ones", [P, P])
        own_s = sb(top, "own_s", [1, ET], I32)
        own_d = sb(top, "own_d", [1, ET], I32)
        meta = sb(top, "meta", [P, ET, 4])
        rel_idx = sb(top, "rel_idx", [P, ET + T], I32)
        src_idx = sb(top, "src_idx", [P, ET + T], I32)
        slot_idx = sb(top, "slot_idx", [P, ET], I32)
        ldst = sb(top, "ldst", [P, ET])
        lsrc = sb(top, "lsrc", [P, ET])
        pads = sb(top, "pads", [P, 2 * NT], I32)
        zero = sb(top, "zero", [P, MW])
        rstd = sb(top, "rstd", [NP, NTP])
        nmr = sb(top, "nmr", [NP, NTP])

        def moments_on_vector(dve, of, st, s_st, s_sq, go):
            v = nc.vector
            for t in range(NTP):
                v.bn_stats(st[:, t, :], of[:, t, 0:D]).then_inc(s_st, 1)
            dve.wait_ge(s_st, NTP)
            go(v.tensor_tensor(rstd[:, :], st[:, :, 1], st[:, :, 4], ALU.subtract))
            go(v.scalar_tensor_tensor(out=rstd[:, :], in0=rstd[:, :], scalar=D / 4, in1=rstd[:, :],
                                      op0=ALU.mult, op1=ALU.mult))
            go(v.tensor_tensor(rstd[:, :], rstd[:, :], st[:, :, 2], ALU.add))
            go(v.tensor_tensor(rstd[:, :], rstd[:, :], st[:, :, 5], ALU.add))
            go(v.tensor_tensor(nmr[:, :], st[:, :, 1], st[:, :, 4], ALU.add))
            v.tensor_scalar(rstd[:, :], rstd[:, :], 1.0 / D, EPS, ALU.mult, ALU.add).then_inc(s_sq, 1)
            dve.wait_ge(s_sq, 2)
            go(v.reciprocal(rstd[:, :], rstd[:, :]))
            go(v.scalar_tensor_tensor(out=nmr[:, :], in0=nmr[:, :], scalar=-0.5, in1=rstd[:, :],
                                      op0=ALU.mult, op1=ALU.mult))

        def order_edges(srcf, dstf, typf, wgt, rows, bins, rank, one, eq, cum, tmp, cnt, total, upto_bin, first, before,
                        p_small, unordered):
            B = 25
            U = 16
            R = EC // U
            with ExitStack() as c:
                slots = sb(c, "slots", [P, EC], I32)
                idx = sb(c, "so_idx", [P, U], I32)
                row = sb(c, "so_row", [P, U, 4])
                s_ch, s_cnt, s_pe, staged, freed, scattered, begun, s_back = (
                    sem(c, "so_" + n) for n in "ch cnt pe staged freed scattered begun back".split())

                def sort_on_vector(dve, go, digit):
                    v = nc.vector

                    def divide(to, of):
                        go(v.tensor_scalar(to[:, :], of[:, :], 1.0 / B, -(B // 2) / B, ALU.mult, ALU.add))
                        go(v.tensor_scalar(to[:, :], to[:, :], MAGIC, -MAGIC, ALU.add, ALU.add))

                    go(v.tensor_copy(bins[:, :], dstf[:, :]))
                    for _ in range(digit):
                        divide(tmp, bins)
                        go(v.tensor_copy(bins[:, :], tmp[:, :]))
                    if digit < 2:
                        divide(tmp, bins)
                        go(v.scalar_tensor_tensor(out=bins[:, :], in0=tmp[:, :], scalar=float(-B), in1=bins[:, :],
                                                  op0=ALU.mult, op1=ALU.add))
                    for k, of in enumerate((srcf, dstf, typf, wgt)):
                        go(v.tensor_copy(rows[:, :, k], of[:, :]))
                    go(v.memset(rank[:, :], 0.0))
                    n0 = go.n
                    with dve.Fori(0, B) as b:
                        at = b * 5 + n0
                        v.tensor_scalar(eq[:, :], bins[:, :], iota_f[:, bass.ds(b, 1)], None, ALU.is_equal).then_inc(s_ch, 1)
                        dve.wait_ge(s_ch, at + 1)
                        v.tensor_tensor_scan(cum[:, :], one[:, :], eq[:, :], 0.0, ALU.mult, ALU.add).then_inc(s_ch, 1)
                        dve.wait_ge(s_ch, at + 2)
                        v.tensor_copy(cnt[:, 0, bass.ds(b, 1)], cum[:, EC - 1:EC]).then_inc(s_ch, 1)
                        v.tensor_tensor(tmp[:, :], eq[:, :], cum[:, :], ALU.mult).then_inc(s_ch, 1)
                        dve.wait_ge(s_ch, at + 4)
                        v.tensor_tensor(rank[:, :], rank[:, :], tmp[:, :], ALU.add).then_inc(s_ch, 1)
                        dve.wait_ge(s_ch, at + 5)
                    go.n = n0 + 5 * B
                    dve.sem_inc(s_cnt, 1)
                    dve.wait_ge(s_pe, digit + 1)
                    go(v.tensor_copy(total[:, :], p_small[:, 32:32 + B]))
                    go(v.tensor_tensor_scan(upto_bin[:, :], one[:, 0:B], total[:, :], 0.0, ALU.mult, ALU.add))
                    go(v.tensor_tensor(first[:, :], upto_bin[:, :], total[:, :], ALU.subtract))
                    go(v.tensor_tensor(first[:, :], first[:, :], p_small[:, 0:B], ALU.add))
                    go(v.tensor_scalar(first[:, :], first[:, :], -1.0, None, ALU.add))
                    n1 = go.n
                    with dve.Fori(0, B) as b:
                        v.tensor_scalar(tmp[:, :], bins[:, :], iota_f[:, bass.ds(b, 1)], first[:, bass.ds(b, 1)],
                                        ALU.is_equal, ALU.mult).then_inc(s_ch, 1)
                        dve.wait_ge(s_ch, b * 2 + (n1 + 1))
                        v.tensor_tensor(rank[:, :], rank[:, :], tmp[:, :], ALU.add).then_inc(s_ch, 1)
                        dve.wait_ge(s_ch, b * 2 + (n1 + 2))
                    go.n = n1 + 2 * B
                    go(v.tensor_copy(slots[:, :], rank[:, :]))
                    with dve.Fori(0, R) as it:
                        dve.wait_ge(freed, it + (digit * R + 1))
                        at = bass.ds(it * U, U)
                        v.tensor_copy(idx[:, :], slots[:, at]).then_inc(staged, 1)
                        v.tensor_copy(row[:, :, :], rows[:, at, :]).then_inc(staged, 1)
                    dve.wait_ge(s_back, 16 * (digit + 1))
                    for k, to in enumerate((srcf, dstf, typf, wgt)):
                        go(v.tensor_copy(to[:, :], rows[:, :, k]))

                with nc.Block() as block:
                    @block.vector
                    def _(dve):
                        go = Link(dve, s_ch)
                        flag = dve.value_load(unordered[0:1, 0:1], min_val=0, max_val=1)
                        with dve.If(flag == 1):
                            for digit in range(3):
                                sort_on_vector(dve, go, digit)

                    @block.tensor
                    def _(pe):
                        flag = pe.value_load(unordered[0:1, 0:1], min_val=0, max_val=1)
                        with pe.If(flag == 1):
                            for digit in range(3):
                                pe.wait_ge(s_cnt, digit + 1)
                                nc.tensor.matmul(p_small[:, 0:B], before[:, :], cnt[:, 0, :], start=True, stop=True)
                                nc.tensor.matmul(p_small[:, 32:32 + B], ones[:, :], cnt[:, 0, :], start=True, stop=True
                                                 ).then_inc(s_pe, 1)

                    @block.gpsimd
                    def _(pool):
                        g = nc.gpsimd
                        flag = pool.value_load(unordered[0:1, 0:1], min_val=0, max_val=1)
                        with pool.If(flag == 1):
                            pool.sem_inc(freed, 1)
                            for digit in range(3):
                                with pool.Fori(0, R) as it:
                                    pool.wait_ge(staged, it * 2 + (2 * digit * R + 2))
                                    pool.sem_inc(begun, 1)
                                    for i in range(U):
                                        g.indirect_dma_start(ordered, bass.IndirectOffsetOnAxis(ap=idx[:, i:i + 1], axis=0),
                                                             row[:, i, :], None).then_inc(scattered, 16)
                                    pool.wait_ge(scattered, it * (16 * U) + (16 * U * (digit * R + 1)))
                                    pool.sem_inc(freed, 1)
                                g.dma_start(rows[:, :, :].rearrange("p e f -> p (e f)"),
                                            ordered.rearrange("(p e) f -> p (e f)", p=P)).then_inc(s_back, 16)
                            pool.wait_ge(s_back, 16 * 3)

        def constants_and_edges():
            with ExitStack() as c:
                srcf, dstf, typf, wgt, bins, bind, eq, cum, tmp, tmp2, rank, one = (
                    sb(c, n, [P, EC]) for n in "srcf dstf typf wgt bins bind eq cum tmp tmp2 rank one".split())
                unordered = sb(c, "unordered", [1, 1], I32)
                falls = sb(c, "falls", [P, 1])
                rows = sb(c, "rows", [P, EC, 4])
                padseq = sb(c, "padseq", [P, P])
                before = sb(c, "before", [P, P])
                upto = sb(c, "upto", [P, P])
                iota_j = sb(c, "iota_j", [P, ET])
                cnt = sb(c, "cnt", [P, 2, NT])
                tiles_of = sb(c, "tiles_of", [P, NT])
                tiles_end = sb(c, "tiles_end", [P, NT])
                first = sb(c, "first", [P, NT])
                cols = sb(c, "cols", [NT, 8])
                ge_s, ge_d = sb(c, "ge_s", [NT, ET]), sb(c, "ge_d", [NT, ET])
                p_small = ps(c, "p_small", [P, 512])
                p_col = ps(c, "p_col", [P, 512])
                p_own_s = ps(c, "p_own_s", [P, 512])
                p_own_d = ps(c, "p_own_d", [P, 512])
                p_tr = ps(c, "p_tr", [P, 4, P])
                p_out = (p_own_s, p_own_d)
                p_meta = [ps(c, f"p_meta{i}", [P, 4, P]) for i in range(2)]
                q = ET // 4
                blocks = sb(c, "blocks", [q, 4, P * 4])
                block_of = sb(c, "block_of", [q, 4], I32)
                block_f = sb(c, "block_f", [q, 4])
                tile_no = sb(c, "tile_no", [q, 4])
                pad_f = sb(c, "pad_f", [P, 2 * NT])
                pad_ok = sb(c, "pad_ok", [P, NT])
                own_rep = sb(c, "own_rep", [P, ET])
                srce, owned, work, dst_of = (sb(c, n, [P, ET]) for n in "srce owned work dst_of".split())
                seqt = sb(c, "seqt", [ET // 4, 2, 4, P])
                w0 = sb(c, "w0", [P, 2, D])
                stats = sb(c, "stats0", [NP, NTP, 6])
                h = sb(c, "h0", [NP, 2, D])
                hT = sb(c, "hT0", [P, 2, 2, NP])
                s_w0, s_st, s_sq, s_mom, s_pads, s_padded, s_acc = (
                    sem(c, "e_" + n) for n in "w0 st sq mom pads padded acc".split())
                h_made, turned, hT_made, made, taken = ([sem(c, f"e_{n}{s}") for s in range(2)]
                                                        for n in "h_made turned hT_made made taken".split())
                srcn, dstn, typn, nextn = (sb(c, n, [P, EC], I32) for n in ("srcn", "dstn", "typn", "nextn"))
                s_load, s_fall, s_ch0 = (sem(c, "e_" + n) for n in "load fall ch0".split())
                (s_set, s_in, s_const, s_ch, s_pe, s_cnt, s_end, s_rows, s_seq, s_x, s_blk, s_off, s_ready, s_tr, s_trc,
                 s_fill, s_m, s_mc) = (sem(c, "e_" + n) for n in
                            "set in const ch pe cnt end rows seq x blk off ready tr trc fill m mc".split())

                with nc.Block() as block:
                    @block.gpsimd
                    def _(pool):
                        g = nc.gpsimd
                        k = Link(pool, s_const)
                        exact = dict(allow_small_or_imprecise_dtypes=True)
                        k(g.iota(iota_f[:, :], [[1, P]], base=0, channel_multiplier=0, **exact))
                        k(g.iota(iota_p[:, :], [[0, 1]], base=0, channel_multiplier=1, **exact))
                        k(g.iota(iota_j[:, :], [[1, ET]], base=0, channel_multiplier=0, **exact))
                        k(g.iota(tile_no[:, :], [[q, 4]], base=0, channel_multiplier=1, **exact))
                        k(g.memset(ident[:, :], 0.0))
                        k(g.memset(ones[:, :], 1.0))
                        k(g.affine_select(out=before[:, :], in_=ones[:, :], pattern=[[1, P]], compare_op=ALU.is_gt,
                                          fill=0.0, base=0, channel_multiplier=-1))
                        k(g.affine_select(out=upto[:, :], in_=ones[:, :], pattern=[[1, P]], compare_op=ALU.is_ge,
                                          fill=0.0, base=0, channel_multiplier=-1))
                        k(g.affine_select(out=ident[:, :], in_=ident[:, :], pattern=[[1, P]], compare_op=ALU.not_equal,
                                          fill=1.0, base=0, channel_multiplier=-1))

                    @block.sync
                    def _(sp):
                        last = (P - 1) * EC
                        sp.wait_ge(s_load, 1)
                        for a, to in ((src, srcn), (dst, dstn), (edge_type_8, typn), (edge_weight, wgt)):
                            sp.dma_start(to[0:P - 1, :], a[0:last].rearrange("(p e) -> p e", e=EC)).then_inc(s_in, 16)
                            sp.dma_start(to[P - 1:P, 0:E - last], a[last:E].rearrange("(p e) -> p e", p=1)).then_inc(s_in, 16)
                        sp.dma_start(nextn[0:P - 1, :], dst[1:last + 1].rearrange("(p e) -> p e", e=EC)).then_inc(s_in, 16)
                        sp.dma_start(nextn[P - 1:P, 0:E - last - 1], dst[last + 1:E].rearrange("(p e) -> p e", p=1)).then_inc(s_in, 16)

                    @block.tensor
                    def _(pe):
                        pe.wait_ge(s_const, 9)
                        pe.wait_ge(s_fall, 1)
                        nc.tensor.matmul(p_small[0:1, 0:1], falls[:, :], ones[:, 0:1], start=True, stop=True).then_inc(s_fall, 1)

                    @block.vector
                    def _(dve):
                        v = nc.vector
                        go = Link(dve, s_ch0)
                        go(v.memset(srcn[:, :], 4095))
                        go(v.memset(dstn[:, :], 4095))
                        go(v.memset(nextn[:, :], 4095))
                        go(v.memset(typn[:, :], 0))
                        go(v.memset(one[:, :], 1.0))
                        v.memset(wgt[:, :], 0.0).then_inc(s_load, 1)
                        dve.wait_ge(s_load, 1)
                        dve.wait_ge(s_in, 16 * 10)
                        go(v.tensor_copy(srcf[:, :], srcn[:, :]))
                        go(v.tensor_copy(dstf[:, :], dstn[:, :]))
                        go(v.tensor_copy(typf[:, :], typn[:, :]))
                        go(v.tensor_copy(tmp[:, :], nextn[:, :]))
                        go(v.tensor_tensor(eq[:, :], dstf[:, :], tmp[:, :], ALU.is_gt))
                        v.tensor_reduce(falls[:, :], eq[:, :], AX.X, ALU.add).then_inc(s_fall, 1)
                        dve.wait_ge(s_fall, 2)
                        go(v.tensor_scalar(unordered[:, :], p_small[0:1, 0:1], 1.0, None, ALU.min))
                order_edges(srcf, dstf, typf, wgt, rows, bins, rank, one, eq, cum, tmp, cnt, tiles_of, tiles_end, first, before,
                            p_small, unordered)
                with nc.Block() as block:
                    @block.gpsimd
                    def _(pool):
                        g = nc.gpsimd
                        g.memset(acc[:, :, :], 0.0).then_inc(s_acc, 1)
                        pool.wait_ge(s_pads, 1)
                        for i in range(2 * NT):
                            g.indirect_dma_start(by_src, bass.IndirectOffsetOnAxis(ap=pads[:, i:i + 1], axis=0), zero[:, :], None,
                                                 bounds_check=ET * P - 1, oob_is_err=False).then_inc(s_padded, 16)
                        pool.wait_ge(s_off, 1)
                        pool.wait_ge(s_rows, 16)
                        for i in range(4):
                            g.indirect_dma_start(blocks[:, i, :], None, edges,
                                                 bass.IndirectOffsetOnAxis(ap=block_of[:, i:i + 1], axis=0)).then_inc(s_blk, 16)
                        pool.wait_ge(s_padded, 16 * 2 * NT)

                    @block.scalar
                    def _(act):
                        for s in range(2):
                            act.sem_inc(hT_made[s], 1)
                            act.sem_inc(taken[s], 1)
                        act.wait_ge(s_sq, 1)
                        nc.scalar.activation(rstd[:, :], rstd[:, :], ACT.Sqrt).then_inc(s_sq, 1)
                        act.wait_ge(s_mom, 1)
                        with act.Fori(0, NTP // 2) as it:
                            for s in range(2):
                                at = bass.ds(it * 2 + s, 1)
                                act.wait_ge(turned[s], it + 1)
                                nc.scalar.activation(h[:, s, :], X[:, at, :].rearrange("p t f -> p (t f)"), ACT.Relu,
                                                     bias=nmr[:, at], scale=rstd[:, at]).then_inc(h_made[s], 1)
                            for s in range(2):
                                act.wait_ge(turned[s], it + 2)
                                act.wait_ge(made[s], it + 1)
                                nc.scalar.activation(hT[:, s, :, :], p_meta[s][:, 0:2, 0:NP], ACT.Copy).then_inc(hT_made[s], 1)
                            for s in range(2):
                                act.wait_ge(made[s], it + 2)
                                nc.scalar.activation(table[:, bass.ds(it * 2 + s, 1), :].rearrange("p t f -> p (t f)"),
                                                     p_out[s][0:NP, 0:D], ACT.Copy).then_inc(taken[s], 1)

                    @block.sync
                    def _(sp):
                        sp.wait_ge(s_set, 1)
                        sp.dma_start(w0[:, :, :], L0_gnn_weight.rearrange("(k p) n -> p k n", p=P)).then_inc(s_w0, 16)
                        sp.dma_start(X[:, 0:NT, :], x.rearrange("(t p) f -> p t f", p=NP)).then_inc(s_x, 16)
                        sp.dma_start(dst_seq[0:P].rearrange("(p e) -> p e", p=1), padseq[0:1, :]).then_inc(s_seq, 16)
                        tail = SQ - ET + 1
                        sp.dma_start(dst_seq[P + ET * P:P + ET * P + tail * P].rearrange("(p e) -> p e", e=P),
                                     padseq[0:tail, :]).then_inc(s_seq, 16)
                        sp.dma_start(score_rows[ET * H:SQ * H, :], zero[0:(SQ - ET) * H, 0:P]).then_inc(s_seq, 16)
                        sp.wait_ge(s_fill, 1)
                        sp.dma_start(edges.rearrange("b (e f) -> (b e f)", f=4).rearrange("(p w) -> p w", p=P),
                                     rows[:, :, :].rearrange("p e f -> p (e f)")).then_inc(s_rows, 16)
                        for k, seq, at in ((0, dst_seq, P), (1, ldst_seq, 0)):
                            sp.wait_ge(s_trc, k + 1)
                            for i in range(4):
                                sp.dma_start(seq[at + i * q * P:at + (i + 1) * q * P].rearrange("(p e) -> p e", e=P),
                                             seqt[:, k, i, :]).then_inc(s_seq, 16)
                        sp.wait_ge(s_x, 16)
                        sp.wait_ge(s_seq, 16 * (3 + 8))

                    @block.tensor
                    def _(pe):
                        mm = nc.tensor.matmul
                        for s in range(2):
                            pe.sem_inc(turned[s], 1)
                            pe.sem_inc(made[s], 1)
                        pe.wait_ge(s_w0, 16)
                        with pe.Fori(0, NTP // 2) as it:
                            for s in range(2):
                                pe.wait_ge(h_made[s], it + 1)
                                pe.wait_ge(hT_made[s], it + 1)
                                for k in range(2):
                                    ins = nc.tensor.transpose(p_meta[s][:, k, 0:NP], h[:, s, k * P:(k + 1) * P], ident[0:NP, 0:NP])
                                ins.then_inc(turned[s], 1)
                            for s in range(2):
                                pe.wait_ge(hT_made[s], it + 2)
                                pe.wait_ge(taken[s], it + 1)
                                for k in range(2):
                                    ins = mm(p_out[s][0:NP, 0:D], hT[:, s, k, :], w0[:, k, :], start=k == 0, stop=k == 1)
                                ins.then_inc(made[s], 1)
                        for s in range(2):
                            pe.wait_ge(taken[s], NTP // 2 + 1)
                            pe.wait_ge(hT_made[s], NTP // 2 + 1)
                        pe.wait_ge(s_cnt, 1)
                        mm(p_small[:, 0:NT], before[:, :], cnt[:, 0, :], start=True, stop=True)
                        mm(p_small[:, 32:32 + NT], ones[:, :], cnt[:, 0, :], start=True, stop=True)
                        mm(p_col[0:NT, 0:1], cnt[:, 0, :], ones[:, 0:1], start=True, stop=True)
                        mm(p_col[0:NT, 1:2], cnt[:, 1, :], ones[:, 0:1], start=True, stop=True).then_inc(s_pe, 1)
                        pe.wait_ge(s_end, 1)
                        mm(p_col[0:NT, 4:5], before[0:NT, 0:NT], cols[:, 1:2], start=True, stop=True).then_inc(s_pe, 1)
                        pe.wait_ge(s_end, 2)
                        mm(p_col[0:NT, 2:4], upto[0:NT, 0:NT], cols[:, 2:4], start=True, stop=True).then_inc(s_pe, 1)
                        pe.wait_ge(s_end, 3)
                        for i in range(4):
                            mm(p_col[0:q, 8 + i:9 + i], ge_d[:, i * q:(i + 1) * q], cols[:, 4:5], start=True, stop=True)
                        mm(p_own_s[:, 0:ET], ones[0:NT, :], ge_s[:, :], start=True, stop=True)
                        mm(p_own_d[:, 0:ET], ones[0:NT, :], ge_d[:, :], start=True, stop=True).then_inc(s_pe, 1)
                        pe.wait_ge(s_blk, 64)
                        for i in range(4):
                            if i >= 2:
                                pe.wait_ge(s_mc, i - 1)
                            for f in range(4):
                                ins = nc.tensor.transpose(p_meta[i % 2][:, f, 0:q], blocks[:, i, f:P * 4:4], ident[0:q, 0:q])
                            ins.then_inc(s_m, 1)
                        for k, a in ((0, dst_of), (1, ldst)):
                            pe.wait_ge(s_ready, 1)
                            if k:
                                pe.wait_ge(s_trc, 1)
                            for i in range(4):
                                ins = nc.tensor.transpose(p_tr[0:q, i, :], a[:, i * q:(i + 1) * q], ident[:, :])
                            ins.then_inc(s_tr, 1)

                    @block.vector
                    def _(dve):
                        v = nc.vector
                        go = Link(dve, s_ch)
                        go(v.memset(padseq[:, :], -1.0))
                        go(v.memset(zero[:, 0:D], 0.0))
                        v.memset(zero[:, D:MW], -1.0).then_inc(s_set, 1)
                        dve.wait_ge(s_set, 1)
                        go(v.memset(X[:, NT, :], 0.0))
                        dve.wait_ge(s_x, 16)
                        moments_on_vector(dve, X, stats, s_st, s_sq, go)
                        dve.sem_inc(s_mom, 1)
                        go(v.memset(rank[:, :], 0.0))
                        for f, b in ((srcf, bins), (dstf, bind)):
                            go(v.tensor_scalar(b[:, :], f[:, :], 1.0 / NP, -(NP // 2) / NP, ALU.mult, ALU.add))
                            go(v.tensor_scalar(b[:, :], b[:, :], MAGIC, -MAGIC, ALU.add, ALU.add))
                        go(v.scalar_tensor_tensor(out=tmp[:, :], in0=srcf[:, :], scalar=float(H), in1=typf[:, :],
                                                  op0=ALU.mult, op1=ALU.add))
                        go(v.tensor_scalar(rows[:, :, 0], tmp[:, :], float(N * H - 1), None, ALU.min))
                        go(v.tensor_copy(rows[:, :, 1], dstf[:, :]))
                        go(v.tensor_copy(rows[:, :, 2], wgt[:, :]))
                        n0 = go.n
                        with dve.Fori(0, NT) as b:
                            at = b * 6 + n0
                            tile = iota_f[:, bass.ds(b, 1)]
                            v.tensor_scalar(eq[:, :], bins[:, :], tile, None, ALU.is_equal).then_inc(s_ch, 1)
                            v.tensor_scalar(tmp2[:, :], bind[:, :], tile, 0.0, ALU.is_equal, ALU.add,
                                            accum_out=cnt[:, 1, bass.ds(b, 1)]).then_inc(s_ch, 1)
                            dve.wait_ge(s_ch, at + 2)
                            v.tensor_tensor_scan(cum[:, :], one[:, :], eq[:, :], 0.0, ALU.mult, ALU.add).then_inc(s_ch, 1)
                            dve.wait_ge(s_ch, at + 3)
                            v.tensor_copy(cnt[:, 0, bass.ds(b, 1)], cum[:, EC - 1:EC]).then_inc(s_ch, 1)
                            v.tensor_tensor(tmp[:, :], eq[:, :], cum[:, :], ALU.mult).then_inc(s_ch, 1)
                            dve.wait_ge(s_ch, at + 5)
                            v.tensor_tensor(rank[:, :], rank[:, :], tmp[:, :], ALU.add).then_inc(s_ch, 1)
                            dve.wait_ge(s_ch, at + 6)
                        go.n = n0 + NT * 6
                        dve.sem_inc(s_cnt, 1)
                        dve.wait_ge(s_pe, 1)
                        up = (P - 1) / 2 / P
                        go(v.tensor_copy(cols[:, 0:2], p_col[0:NT, 0:2]))
                        go(v.tensor_scalar(cols[:, 2:3], cols[:, 0:1], 1.0 / P, up, ALU.mult, ALU.add))
                        v.tensor_scalar(cols[:, 2:3], cols[:, 2:3], MAGIC, -MAGIC, ALU.add, ALU.add).then_inc(s_end, 1)
                        dve.wait_ge(s_end, 1)
                        dve.wait_ge(s_pe, 2)
                        go(v.tensor_copy(cols[:, 5:6], p_col[0:NT, 4:5]))
                        go(v.tensor_tensor(cols[:, 6:7], cols[:, 5:6], cols[:, 1:2], ALU.add))
                        go(v.tensor_scalar(cols[:, 7:8], cols[:, 6:7], -1.0, None, ALU.add))
                        go(v.tensor_scalar(cols[:, 5:8], cols[:, 5:8], 1.0 / P, -up, ALU.mult, ALU.add))
                        go(v.tensor_scalar(cols[:, 5:8], cols[:, 5:8], MAGIC, -MAGIC, ALU.add, ALU.add))
                        go(v.tensor_tensor(cols[:, 3:4], cols[:, 7:8], cols[:, 5:6], ALU.subtract))
                        go(v.tensor_scalar(cols[:, 3:4], cols[:, 3:4], 1.0, None, ALU.add))
                        go(v.tensor_scalar(cols[:, 7:8], cols[:, 1:2], 0.0, None, ALU.is_gt))
                        go(v.tensor_tensor(cols[:, 3:4], cols[:, 3:4], cols[:, 7:8], ALU.mult))
                        go(v.tensor_tensor(cols[:, 4:5], cols[:, 6:7], cols[:, 5:6], ALU.subtract))
                        v.tensor_tensor(cols[:, 4:5], cols[:, 4:5], cols[:, 3:4], ALU.subtract).then_inc(s_end, 1)
                        dve.wait_ge(s_end, 2)
                        dve.wait_ge(s_pe, 3)
                        go(v.tensor_copy(cols[:, 6:8], p_col[0:NT, 2:4]))
                        go(v.tensor_scalar(ge_s[:, :], iota_j[0:NT, :], cols[:, 6:7], None, ALU.is_ge))
                        v.tensor_scalar(ge_d[:, :], iota_j[0:NT, :], cols[:, 7:8], None, ALU.is_ge).then_inc(s_end, 1)
                        dve.wait_ge(s_end, 3)
                        go(v.tensor_scalar(tiles_of[:, :], p_small[:, 32:32 + NT], 1.0 / P, up, ALU.mult, ALU.add))
                        go(v.tensor_scalar(tiles_of[:, :], tiles_of[:, :], MAGIC, -MAGIC, ALU.add, ALU.add))
                        go(v.tensor_tensor_scan(tiles_end[:, :], one[:, 0:NT], tiles_of[:, :], 0.0, ALU.mult, ALU.add))
                        go(v.tensor_scalar(pad_f[:, 0:NT], tiles_end[:, :], float(P), float(-P), ALU.mult, ALU.add))
                        go(v.tensor_scalar(pad_f[:, 0:NT], pad_f[:, 0:NT], iota_p[:, :], None, ALU.add))
                        go(v.tensor_tensor(first[:, :], tiles_end[:, :], tiles_of[:, :], ALU.subtract))
                        go(v.scalar_tensor_tensor(out=first[:, :], in0=first[:, :], scalar=float(P),
                                                  in1=p_small[:, 32:32 + NT], op0=ALU.mult, op1=ALU.add))
                        go(v.tensor_tensor(pad_ok[:, :], pad_f[:, 0:NT], first[:, :], ALU.is_ge))
                        go(v.scalar_tensor_tensor(out=pad_f[:, 0:NT], in0=pad_f[:, 0:NT], scalar=float(-ET * P),
                                                  in1=pad_ok[:, :], op0=ALU.add, op1=ALU.mult))
                        go(v.tensor_scalar(pad_f[:, 0:NT], pad_f[:, 0:NT], float(ET * P), None, ALU.add))
                        go(v.tensor_scalar(pad_f[:, NT:2 * NT], iota_f[:, 0:NT], tiles_end[:, NT - 1:NT], float(P),
                                           ALU.add, ALU.mult))
                        go(v.tensor_scalar(pad_f[:, NT:2 * NT], pad_f[:, NT:2 * NT], iota_p[:, :], None, ALU.add))
                        v.tensor_copy(pads[:, :], pad_f[:, :]).then_inc(s_pads, 1)
                        go(v.tensor_tensor(first[:, :], tiles_end[:, :], tiles_of[:, :], ALU.subtract))
                        go(v.tensor_scalar(first[:, :], first[:, :], float(P), -1.0, ALU.mult, ALU.add))
                        go(v.tensor_tensor(first[:, :], first[:, :], p_small[:, 0:NT], ALU.add))
                        n1 = go.n
                        with dve.Fori(0, NT) as b:
                            v.tensor_scalar(tmp[:, :], bins[:, :], iota_f[:, bass.ds(b, 1)], first[:, bass.ds(b, 1)],
                                            ALU.is_equal, ALU.mult).then_inc(s_ch, 1)
                            dve.wait_ge(s_ch, b * 2 + (n1 + 1))
                            v.tensor_tensor(rank[:, :], rank[:, :], tmp[:, :], ALU.add).then_inc(s_ch, 1)
                            dve.wait_ge(s_ch, b * 2 + (n1 + 2))
                        go.n = n1 + 2 * NT
                        v.tensor_copy(rows[:, :, 3], rank[:, :]).then_inc(s_fill, 1)
                        dve.wait_ge(s_pe, 4)
                        go(v.tensor_tensor(block_f[:, :], tile_no[:, :], p_col[0:q, 8:12], ALU.add))
                        v.tensor_scalar(block_of[:, :], block_f[:, :], float(EC - 1), None, ALU.min).then_inc(s_off, 1)
                        go(v.tensor_copy(own_s[:, :], p_own_s[0:1, 0:ET]))
                        go(v.tensor_copy(own_d[:, :], p_own_d[0:1, 0:ET]))
                        go(v.tensor_copy(own_rep[:, :], p_own_d[:, 0:ET]))
                        for i in range(4):
                            dve.wait_ge(s_m, i + 1)
                            v.tensor_copy(meta[:, i * q:(i + 1) * q, :].rearrange("p j f -> p f j"), p_meta[i % 2][:, :, 0:q]
                                          ).then_inc(s_mc, 1)
                        dve.wait_ge(s_mc, 4)
                        go(v.tensor_copy(rel_idx[:, 0:ET], meta[:, :, 0]))
                        go(v.memset(rel_idx[:, ET:ET + T], 0))
                        go(v.tensor_scalar(srce[:, :], meta[:, :, 0], 1.0 / H, -(H - 1) / 2 / H, ALU.mult, ALU.add))
                        go(v.tensor_scalar(srce[:, :], srce[:, :], MAGIC, -MAGIC, ALU.add, ALU.add))
                        go(v.tensor_copy(src_idx[:, 0:ET], srce[:, :]))
                        go(v.memset(src_idx[:, ET:ET + T], 0))
                        go(v.scalar_tensor_tensor(out=ldst[:, :], in0=own_rep[:, :], scalar=float(-NP), in1=meta[:, :, 1],
                                                  op0=ALU.mult, op1=ALU.add))
                        go(v.tensor_scalar(owned[:, :], ldst[:, :], 0.0, None, ALU.is_ge))
                        go(v.scalar_tensor_tensor(out=owned[:, :], in0=ldst[:, :], scalar=float(NP), in1=owned[:, :],
                                                  op0=ALU.is_lt, op1=ALU.mult))
                        go(v.scalar_tensor_tensor(out=dst_of[:, :], in0=meta[:, :, 1], scalar=1.0, in1=owned[:, :],
                                                  op0=ALU.add, op1=ALU.mult))
                        v.tensor_scalar(dst_of[:, :], dst_of[:, :], -1.0, None, ALU.add).then_inc(s_ready, 1)
                        dve.wait_ge(s_ready, 1)
                        go(v.tensor_scalar(work[:, :], srce[:, :], 1.0 / NP, -(NP // 2) / NP, ALU.mult, ALU.add))
                        go(v.tensor_scalar(work[:, :], work[:, :], MAGIC, -MAGIC, ALU.add, ALU.add))
                        go(v.scalar_tensor_tensor(out=lsrc[:, :], in0=work[:, :], scalar=float(-NP), in1=srce[:, :],
                                                  op0=ALU.mult, op1=ALU.add))
                        go(v.tensor_scalar(work[:, :], meta[:, :, 3], float(-ET * P), None, ALU.add))
                        go(v.tensor_tensor(work[:, :], work[:, :], owned[:, :], ALU.mult))
                        go(v.tensor_scalar(slot_idx[:, :], work[:, :], float(ET * P), None, ALU.add))
                        for k in range(2):
                            dve.wait_ge(s_tr, k + 1)
                            v.tensor_copy(seqt[:, k, :, :], p_tr[0:q, :, :]).then_inc(s_trc, 1)

        def moments(of, tag, loads=(), sums=None, clear_sums=False):
            with ExitStack() as c:
                st = sb(c, tag + "st", [NP, NTP, 6])
                s_st, s_sq, s_ch, s_l, s_a = (sem(c, tag + n) for n in ("s_st", "s_sq", "s_ch", "s_l", "s_a"))
                with nc.Block() as block:
                    if loads:
                        @block.sync
                        def _(sp):
                            for to, from_ in loads:
                                sp.dma_start(to, from_).then_inc(s_l, 16)
                            sp.wait_ge(s_l, 16 * len(loads))

                    if sums is not None or clear_sums:
                        @block.gpsimd
                        def _(pool):
                            if sums is not None:
                                pool.wait_ge(s_a, 1)
                            nc.gpsimd.memset(acc[:, :, :], 0.0).then_inc(s_a, 1)

                    @block.vector
                    def _(dve):
                        v = nc.vector
                        if sums is not None:
                            v.tensor_tensor(of[:, 0:NT, :], of[:, 0:NT, :], sums[:, 0:NT, 0:D], ALU.add).then_inc(s_a, 1)
                            dve.wait_ge(s_a, 1)
                        moments_on_vector(dve, of, st, s_st, s_sq, Link(dve, s_ch))

                    @block.scalar
                    def _(act):
                        act.wait_ge(s_sq, 1)
                        nc.scalar.activation(rstd[:, :], rstd[:, :], ACT.Sqrt).then_inc(s_sq, 1)

        def project(tag, w, width, units, put, store=None, copies=2, stores=1, rows=None):
            with ExitStack() as c:
                h = sb(c, tag + "h", [NP, 2, D])
                hT = sb(c, tag + "hT", [P, 2, 2, NP])
                banks = -(-width // 512)
                pT = [ps(c, f"{tag}pT{s}", [P, 2, 256]) for s in range(2)]
                pO = [ps(c, f"{tag}pO{s}", [P, banks * 512]) for s in range(2)]
                s_h, s_t, s_c, s_o, s_e, s_d = ([sem(c, f"{tag}{n}{s}") for s in range(2)]
                                                for n in ("s_h", "s_t", "s_c", "s_o", "s_e", "s_d"))
                last = NTP // 2 - 1
                with nc.Block() as block:
                    @block.scalar
                    def _(act):
                        for s in range(2):
                            act.sem_inc(s_e[s], 1)

                        def normal(it, s):
                            act.wait_ge(s_t[s], it + 1)
                            at = bass.ds(it * 2 + s, 1)
                            if rows is None:
                                nc.scalar.activation(h[:, s, :], X[:, at, :].rearrange("p t f -> p (t f)"), ACT.Relu,
                                                     bias=nmr[:, at], scale=rstd[:, at]).then_inc(s_h[s], 1)
                            else:
                                nc.scalar.activation(h[:, s, :], rows[:, at, 0:D].rearrange("p t f -> p (t f)"),
                                                     ACT.Copy).then_inc(s_h[s], 1)

                        for s in range(2):
                            normal(0, s)
                        with act.Fori(0, last) as it:
                            for s in range(2):
                                normal(it + 1, s)
                                put("act", act, it, s, pO, s_o, s_e, s_d)
                        for s in range(2):
                            put("act", act, last, s, pO, s_o, s_e, s_d)

                    @block.tensor
                    def _(pe):
                        for s in range(2):
                            pe.sem_inc(s_t[s], 1)
                            pe.sem_inc(s_o[s], 1)

                        def turn(it, s):
                            pe.wait_ge(s_h[s], it + 1)
                            pe.wait_ge(s_c[s], it + 1)
                            for k in range(2):
                                ins = nc.tensor.transpose(pT[s][:, k, 0:NP], h[:, s, k * P:(k + 1) * P], ident[0:NP, 0:NP])
                            ins.then_inc(s_t[s], 1)

                        def multiply(it, s):
                            pe.wait_ge(s_c[s], it + 2)
                            for u in range(units):
                                if units == 2:
                                    z = u
                                    pe.wait_ge(s_e[z], it * 2 + (s + 1))
                                else:
                                    z = s
                                    pe.wait_ge(s_e[z], it * copies + 1)
                                for n0 in range(0, width, 512):
                                    n1 = min(width, n0 + 512)
                                    parts = w(u, n0, n1)
                                    for k, rhs in parts:
                                        ins = nc.tensor.matmul(pO[z][0:NP, n0:n1], hT[:, s, k, :], rhs, start=k == parts[0][0],
                                                               stop=k == parts[-1][0])
                                ins.then_inc(s_o[z], 1)

                        for s in range(2):
                            turn(0, s)
                        with pe.Fori(0, last) as it:
                            for s in range(2):
                                multiply(it, s)
                                turn(it + 1, s)
                        for s in range(2):
                            multiply(last, s)

                    @block.vector
                    def _(dve):
                        for s in range(2):
                            dve.sem_inc(s_c[s], 1)

                        def copy(it, s, first=False):
                            dve.wait_ge(s_t[s], it + 2)
                            if not first:
                                if units == 2:
                                    dve.wait_ge(s_o[1], it * 2 + s)
                                else:
                                    dve.wait_ge(s_o[s], it + 1)
                            nc.vector.tensor_copy(hT[:, s, :, :], pT[s][:, :, 0:NP]).then_inc(s_c[s], 1)

                        for s in range(2):
                            copy(0, s, first=True)
                        with dve.Fori(0, last) as it:
                            for s in range(2):
                                copy(it + 1, s)
                                put("dve", dve, it, s, pO, s_o, s_e, s_d)
                        for s in range(2):
                            put("dve", dve, last, s, pO, s_o, s_e, s_d)

                    if store is not None:
                        @block.sync
                        def _(sp):
                            for s in range(2):
                                sp.sem_inc(s_d[s], 1)
                            with sp.Fori(0, NTP // 2) as it:
                                for s in range(2):
                                    store(sp, it, s, s_e, s_d)
                            for s in range(2):
                                sp.wait_ge(s_d[s], stores * 16 * (NTP // 2) + 1)

        def whole(wt):
            return lambda u, n0, n1: [(k, wt[:, k, n0:n1]) for k in range(2)]

        def layer1_in():
            with ExitStack() as c:
                wt = sb(c, "w1", [P, 2, H, P])
                ry = sb(c, "ry", [NP, 2, H, 2, P])
                s_z = sem(c, "w1z")
                with nc.Block() as block:
                    @block.vector
                    def _(dve):
                        nc.vector.memset(wt[:, :, :, :], 0.0).then_inc(s_z, 1)
                        dve.wait_ge(s_z, 1)
                blocks = L1_gnn_weight.rearrange("r (b i o) -> b i r o", b=H, i=DH)
                moments(X, "a1", [(wt[(b % 4) * DH:(b % 4 + 1) * DH, b // 4, :, (b % 4) * DH:(b % 4 + 1) * DH], blocks[b])
                                  for b in range(H)], acc)

                def w(u, n0, n1):
                    return [(u, wt[:, u, n0 // P:n1 // P, :])]

                def put(who, eng, it, s, pO, made, taken, stored):
                    u = 0 if who == "act" else 1
                    eng.wait_ge(made[u], it * 2 + (s + 2))
                    eng.wait_ge(stored[s], it * 16 + 1)
                    o = ry[:, s, :, u, :]
                    i = pO[u][0:NP, :].rearrange("p (r f) -> p r f", r=H)
                    if u == 0:
                        nc.scalar.activation(o, i, ACT.Copy).then_inc(taken[u], 1)
                    else:
                        nc.vector.tensor_copy(o, i).then_inc(taken[u], 1)

                def store(sp, it, s, taken, stored):
                    for u in range(2):
                        sp.wait_ge(taken[u], it * 2 + (s + 2))
                    sp.dma_start(rel_table[bass.ds((it * 2 + s) * (NP * H), NP * H), :].rearrange("(p r) f -> p (r f)", r=H),
                                 ry[:, s, :, :, :].rearrange("p r k f -> p (r k f)")).then_inc(stored[s], 16)
                project("d1", w, H * P, 2, put, store)

        def layer2_in():
            with ExitStack() as c:
                wt = sb(c, "w2", [P, 2, 3 * D])
                kv = sb(c, "kv", [NP, 2, 2 * D])
                moments(X, "a2", [(wt[:, :, i * D:(i + 1) * D], a.rearrange("(k p) n -> p k n", p=P))
                                  for i, a in enumerate((L2_gnn_Wk, L2_gnn_Wv, L2_gnn_Wq))], acc)

                def put(who, eng, it, s, pO, made, taken, stored):
                    eng.wait_ge(made[s], it + 2)
                    if who == "act":
                        eng.wait_ge(stored[s], it * 32 + 1)
                        nc.scalar.activation(kv[:, s, :], pO[s][0:NP, 0:2 * D], ACT.Copy).then_inc(taken[s], 1)
                    else:
                        nc.vector.tensor_copy(table[:, bass.ds(it * 2 + s, 1), :].rearrange("p t f -> p (t f)"),
                                              pO[s][0:NP, 2 * D:3 * D]).then_inc(taken[s], 1)

                def store(sp, it, s, taken, stored):
                    sp.wait_ge(taken[s], it * 2 + 3)
                    nodes = bass.ds((it * 2 + s) * NP, NP)
                    sp.dma_start(key_table[nodes, :], kv[:, s, 0:D]).then_inc(stored[s], 16)
                    sp.dma_start(value_table[nodes, :], kv[:, s, D:2 * D]).then_inc(stored[s], 16)
                project("d2", whole(wt), 3 * D, 1, put, store, stores=2)

        def layer3_in():
            with ExitStack() as c:
                wt = sb(c, "w3", [P, 2, D + 2 * H])
                av = sb(c, "av", [P, H, 2 * DH])
                wa = sb(c, "wa", [P, H, DH])
                wh = sb(c, "wh", [NP, 2, MW])
                s_ch = sem(c, "w3ch")
                moments(X, "a3", [(wt[:, k, 0:D].rearrange("p (h d) -> p h d", h=H),
                                   L3_gnn_W[:, k * P:(k + 1) * P, :].rearrange("h p d -> p h d")) for k in range(2)]
                        + [(av[:, :, :], L3_gnn_a.partition_broadcast(P))])
                with nc.Block() as block:
                    @block.vector
                    def _(dve):
                        go = Link(dve, s_ch)
                        for k in range(2):
                            for i in range(2):
                                go(nc.vector.tensor_tensor(wa[:, :, :], wt[:, k, 0:D].rearrange("p (h d) -> p h d", h=H),
                                                           av[:, :, i * DH:(i + 1) * DH], ALU.mult))
                                go(nc.vector.tensor_reduce(wt[:, k, D + i * H:D + (i + 1) * H], wa[:, :, :], AX.X, ALU.add))

                def put(who, eng, it, s, pO, made, taken, stored):
                    if who == "act":
                        eng.wait_ge(made[s], it + 2)
                        eng.wait_ge(stored[s], it * 32 + 1)
                        nc.scalar.activation(wh[:, s, :], pO[s][0:NP, 0:MW], ACT.Copy).then_inc(taken[s], 1)
                        nc.scalar.activation(table[:, bass.ds(it * 2 + s, 1), 0:H].rearrange("p t f -> p (t f)"),
                                             pO[s][0:NP, MW:MW + H], ACT.Copy).then_inc(taken[s], 1)

                def store(sp, it, s, taken, stored):
                    sp.wait_ge(taken[s], it * 2 + 3)
                    nodes = bass.ds((it * 2 + s) * NP, NP)
                    sp.dma_start(wh_table[nodes, :], wh[:, s, 0:D]).then_inc(stored[s], 16)
                    sp.dma_start(s1_table[nodes, :], wh[:, s, D:MW]).then_inc(stored[s], 16)
                project("d3", whole(wt), D + 2 * H, 1, put, store, stores=2)

        regs = {e.engine: [e.alloc_register(f"own_{k}_{i}") for i in range(G)]
                for k, e in (("pe", nc.tensor), ("dve", nc.vector))}

        def owners(eng, own, it, q, hi):
            eng.reg_load(regs[eng.engine], own[0:1, bass.ds(it * T + q * G, G)])
            return [eng.snap(r, min_val=0, max_val=hi) for r in regs[eng.engine]]

        def scatter_by_source():
            with ExitStack() as c:
                bl = sb(c, "bl", [NP, NG, G * P])
                oht = sb(c, "oht", [NP, NG, G * P])
                msg = sb(c, "msg", [P, NG, G, MW])
                idx = sb(c, "idx", [P, NG, G], I32)
                counted = sb(c, "sc_counted", [1, NG])
                pE = [ps(c, f"pE{s}", [P, 512]) for s in range(2)]
                bl_in, scattered = ([sem(c, f"sc_{n}{q}") for q in range(NG)] for n in ("bl_in", "scattered"))
                oht_made, idx_made, expanded, messaged, begun = (
                    sem(c, "sc_" + n) for n in "oht_made idx_made expanded messaged begun".split())
                with nc.Block() as block:
                    @block.sync
                    def _(sp):
                        with sp.Fori(0, ITER) as it:
                            for q in range(NG):
                                sp.wait_ge(oht_made, it * NG + (q + 1))
                                sp.dma_start(bl[:, q, :], ldst_seq[bass.ds((it * NG + q) * (G * P), G * P)]
                                             .partition_broadcast(NP)).then_inc(bl_in[q], 16)

                    @block.vector
                    def _(dve):
                        v = nc.vector
                        dve.sem_inc(oht_made, NG)
                        with dve.Fori(0, ITER) as it:
                            for q in range(NG):
                                dve.wait_ge(bl_in[q], it * 16 + 16)
                                dve.wait_ge(expanded, it * T + (q + 1) * G)
                                v.tensor_scalar(oht[:, q, :], bl[:, q, :], iota_p[0:NP, :], None,
                                                ALU.is_equal).then_inc(oht_made, 1)
                                dve.wait_ge(scattered[q], it * (16 * G) + 16)
                                j = bass.ds((it * NG + q) * G, G)
                                v.tensor_copy(msg[:, q, :, D:D + 1], lsrc[:, j].unsqueeze(2)).then_inc(idx_made, 1)
                                v.tensor_copy(idx[:, q, :], slot_idx[:, j]).then_inc(idx_made, 1)

                    @block.tensor
                    def _(pe):
                        pe.sem_inc(expanded, T)
                        with pe.Fori(0, ITER) as it:
                            for q in range(NG):
                                own = owners(pe, own_d, it, q, NT)
                                pe.wait_ge(oht_made, it * NG + (NG + q + 1))
                                for i in range(G):
                                    n = q * G + i
                                    pe.wait_ge(messaged, it * T + (T + n - 1))
                                    nc.tensor.matmul(pE[n % 2][:, 0:D], oht[:, q, i * P:(i + 1) * P],
                                                     table[:, bass.ds(own[i], 1), :], start=True, stop=True
                                                     ).then_inc(expanded, 1)

                    @block.scalar
                    def _(act):
                        act.sem_inc(messaged, T)
                        with act.Fori(0, ITER) as it:
                            for q in range(NG):
                                act.wait_ge(scattered[q], it * (16 * G) + 16)
                                for i in range(G):
                                    n = q * G + i
                                    act.wait_ge(expanded, it * T + (T + n + 1))
                                    nc.scalar.activation(msg[:, q, i, 0:D], pE[n % 2][:, 0:D], ACT.Copy,
                                                         scale=meta[:, bass.ds(it * T + n, 1), 2]).then_inc(messaged, 1)

                    @block.gpsimd
                    def _(pool):
                        nc.gpsimd.memset(msg[:, :, :, D + 1:MW], 0.0).then_inc(begun, 1)
                        pool.wait_ge(begun, 1)
                        for q in range(NG):
                            nc.gpsimd.dma_start(counted[:, q:q + 1], iota_f[0:1, q:q + 1]).then_inc(scattered[q], 16)
                        with pool.Fori(0, ITER) as it:
                            for q in range(NG):
                                pool.wait_ge(idx_made, it * (2 * NG) + 2 * (q + 1))
                                pool.wait_ge(messaged, it * T + (T + (q + 1) * G))
                                pool.sem_inc(begun, 1)
                                for i in range(G):
                                    nc.gpsimd.indirect_dma_start(
                                        by_src, bass.IndirectOffsetOnAxis(ap=idx[:, q, i:i + 1], axis=0), msg[:, q, i, :], None,
                                        bounds_check=ET * P - 1, oob_is_err=False).then_inc(scattered[q], 16)
                        for q in range(NG):
                            pool.wait_ge(scattered[q], ITER * 16 * G + 16)

        def sum_over_edges(tag, own, gather=None, weighted=False, probs=False):
            width = MW if probs else D
            with ExitStack() as c:
                msg = sb(c, tag + "msg", [P, NG, G, MW])
                oh = sb(c, tag + "oh", [P, T, NP])
                dist = sb(c, tag + "dist", [P, 2, G, NP])
                idx = sb(c, tag + "idx", [P, NG, G], I32)
                prows = sb(c, tag + "prows", [10 * H, 2, P])
                pcols = sb(c, tag + "pcols", [P, T, H])
                paired = width <= 256
                pM = [ps(c, f"{tag}pM{i}", [P, 3 * 512]) for i in range(2)] if paired else [
                    ps(c, f"{tag}pM{i}", [P, 512]) for i in range(G)]

                def product(q, i):
                    return pM[q % 2][0:NP, i * 256:i * 256 + width] if paired else pM[i][0:NP, 0:width]
                pT = [ps(c, f"{tag}pT{i}", [P, 512]) for i in range(2)]
                filled = [sem(c, f"{tag}filled{q}") for q in range(NG)]
                p_in = [sem(c, f"{tag}p_in{k}") for k in range(2)]
                idx_made, oh_made, summed, added, turned, copied, prepared, begun, apart = (
                    sem(c, tag + n) for n in "idx_made oh_made summed added turned copied prepared begun apart".split())
                table_of, index = gather or (None, None)
                fill = 16 * (G if gather else 1)
                with nc.Block() as block:
                    @block.sync
                    def _(sp):
                        if probs or not gather:
                            with sp.Fori(0, ITER) as it:
                                if probs:
                                    for k in range(2):
                                        sp.wait_ge(turned, it * 2 + 1)
                                        sp.dma_start(prows[:, k, :], prob_rows[bass.ds((it * T + k * 10) * H, 10 * H), :]
                                                     ).then_inc(p_in[k], 16)
                                if not gather:
                                    for q in range(NG):
                                        sp.wait_ge(summed, it * T + (q + 1) * G)
                                        sp.dma_start(msg[:, q, :, :], by_src[bass.ds((it * T + q * G) * P, G * P), :]
                                                     .rearrange("(t p) f -> p t f", p=P)).then_inc(filled[q], 16)

                    @block.gpsimd
                    def _(pool):
                        if gather:
                            with pool.Fori(0, ITER) as it:
                                for q in range(NG):
                                    pool.wait_ge(idx_made, it * NG + (q + 1))
                                    pool.wait_ge(summed, it * T + (q + 1) * G)
                                    pool.sem_inc(begun, 1)
                                    for i in range(G):
                                        nc.gpsimd.indirect_dma_start(
                                            msg[:, q, i, 0:D], None, table_of,
                                            bass.IndirectOffsetOnAxis(ap=idx[:, q, i:i + 1], axis=0)).then_inc(filled[q], 16)

                    @block.scalar
                    def _(act):
                        if probs:
                            act.sem_inc(copied, 1)
                            with act.Fori(0, ITER) as it:
                                for k in range(2):
                                    act.wait_ge(turned, it * 2 + (k + 2))
                                    act.wait_ge(prepared, it * NG + (2 * k + 2))
                                    nc.scalar.activation(pcols[:, k * 10:(k + 1) * 10, :].rearrange("p t h -> p (t h)"),
                                                         pT[k][:, 0:10 * H], ACT.Copy).then_inc(copied, 1)

                        if not gather:
                            act.sem_inc(apart, 1)
                            with act.Fori(0, ITER) as it:
                                for q in range(NG):
                                    act.wait_ge(filled[q], it * fill + fill)
                                    act.wait_ge(summed, it * T + (q + 1) * G)
                                    for i in range(G):
                                        ins = nc.scalar.activation(dist[:, q % 2, i, :], iota_f[:, 0:NP], ACT.Abs, scale=-1.0,
                                                                   bias=msg[:, q, i, D:D + 1])
                                    ins.then_inc(apart, 1)
                                    act.wait_ge(apart, it * NG + (q + 2))
                                    nc.scalar.activation(oh[:, q * G:(q + 1) * G, :], dist[:, q % 2, :, :], ACT.Relu, scale=-1.0,
                                                         bias=ones[:, 0:1]).then_inc(oh_made, 1)

                    @block.tensor
                    def _(pe):
                        pe.sem_inc(turned, 1)
                        pe.sem_inc(summed, T)

                        def turn(it, k, first=False):
                            pe.wait_ge(p_in[k], it * 16 + 16)
                            if not first:
                                pe.wait_ge(copied, it * 2 + k)
                            nc.tensor.transpose(pT[k][:, 0:10 * H], prows[:, k, :], ident[0:10 * H, 0:10 * H]).then_inc(turned, 1)

                        def multiply(it, q):
                            pe.wait_ge(filled[q], it * fill + fill)
                            pe.wait_ge(oh_made, it * NG + (q + 1))
                            if paired:
                                pe.wait_ge(added, it * T + (q + 1) * G)
                            for i in range(G):
                                n = q * G + i
                                if not paired:
                                    pe.wait_ge(added, it * T + (n + G + 1))
                                nc.tensor.matmul(product(q, i), oh[:, n, :], msg[:, q, i, 0:width],
                                                 start=True, stop=True).then_inc(summed, 1)

                        if probs:
                            for k in range(2):
                                turn(0, k, first=True)
                        with pe.Fori(0, ITER - 1) as it:
                            for q in range(NG):
                                multiply(it, q)
                                if probs and q in (1, 2):
                                    turn(it + 1, q - 1)
                        for q in range(NG):
                            multiply(ITER - 1, q)

                    @block.vector
                    def _(dve):
                        v = nc.vector

                        def add(it, q):
                            node_tile = owners(dve, own, it, q, NT)
                            if paired:
                                dve.wait_ge(summed, it * T + (T + (q + 1) * G))
                            for i in range(G):
                                n = q * G + i
                                if not paired:
                                    dve.wait_ge(summed, it * T + (T + n + 1))
                                dve.wait_ge(added, it * T + (n + 2 * G))
                                at = acc[:, bass.ds(node_tile[i], 1), 0:width]
                                v.tensor_tensor(at, at, product(q, i).unsqueeze(1), ALU.add).then_inc(added, 1)
                            if gather:
                                v.tensor_copy(idx[:, q, :], index[:, bass.ds(it * T + (T + q * G), G)]).then_inc(idx_made, 1)

                        def prepare(it, q):
                            at = bass.ds((it * NG + q) * G, G)
                            if probs:
                                dve.wait_ge(filled[q], it * fill + fill)
                                dve.wait_ge(copied, it * 2 + (q // 2 + 2))
                                m = msg[:, q, :, 0:D].rearrange("p g (h d) -> p g h d", h=H)
                                pq = pcols[:, q * G:(q + 1) * G, :]
                                v.tensor_tensor(m, m, pq.unsqueeze(3).to_broadcast([P, G, H, DH]), ALU.mult)
                                v.tensor_copy(msg[:, q, :, D:MW], pq).then_inc(prepared, 1)
                                ins = v.tensor_tensor(oh[:, q * G:(q + 1) * G, :],
                                                      iota_f[:, 0:NP].unsqueeze(1).to_broadcast([P, G, NP]),
                                                      ldst[:, at].unsqueeze(2).to_broadcast([P, G, NP]), ALU.is_equal)
                            elif weighted:
                                for i in range(G):
                                    j = bass.ds(it * T + (q * G + i), 1)
                                    ins = v.tensor_scalar(oh[:, q * G + i, :], iota_f[:, 0:NP], ldst[:, j], meta[:, j, 2],
                                                          ALU.is_equal, ALU.mult)
                            else:
                                return
                            ins.then_inc(oh_made, 1)

                        if gather:
                            for q in range(NG):
                                v.tensor_copy(idx[:, q, :], index[:, q * G:(q + 1) * G]).then_inc(idx_made, 1)
                        dve.sem_inc(added, 2 * G)
                        dve.sem_inc(prepared, NG)
                        prepare(0, 0)
                        with dve.Fori(0, ITER - 1) as it:
                            for q in range(NG):
                                prepare(*((it, q + 1) if q + 1 < NG else (it + 1, 0)))
                                add(it, q)
                        for q in range(NG):
                            if q + 1 < NG:
                                prepare(ITER - 1, q + 1)
                            add(ITER - 1, q)

        def scores(tag, table_of, width):
            dots = width == D
            with ExitStack() as c:
                bl = sb(c, tag + "bl", [NP, NG, G * P])
                oht = sb(c, tag + "oht", [NP, NG, G * P])
                rows = sb(c, tag + "rows", [P, NG, G, width])
                prod = sb(c, tag + "prod", [P, 2, G, width])
                idx = sb(c, tag + "idx", [P, NG, G], I32)
                sc = sb(c, tag + "sc", [P, T, H])
                srow = sb(c, tag + "srow", [10 * H, 2, P])
                pE = [ps(c, f"{tag}pE{s}", [P, 6 * 256]) for s in range(2)]
                pT = [ps(c, f"{tag}pT{s}", [P, 512]) for s in range(2)]
                bl_in, gathered = ([sem(c, f"{tag}{n}{q}") for q in range(NG)] for n in ("bl_in", "gathered"))
                stored = [sem(c, f"{tag}stored{k}") for k in range(2)]
                oht_made, idx_made, expanded, scored, multiplied, turned, copied, begun = (
                    sem(c, tag + n) for n in "oht_made idx_made expanded scored multiplied turned copied begun".split())
                with nc.Block() as block:
                    @block.sync
                    def _(sp):
                        with sp.Fori(0, ITER) as it:
                            for q in range(NG):
                                sp.wait_ge(oht_made, it * NG + (q + 1))
                                sp.dma_start(bl[:, q, :], ldst_seq[bass.ds((it * NG + q) * (G * P), G * P)]
                                             .partition_broadcast(NP)).then_inc(bl_in[q], 16)

                    @block.gpsimd
                    def _(pool):
                        with pool.Fori(0, ITER) as it:
                            for q in range(NG):
                                pool.wait_ge(idx_made, it * NG + (q + 1))
                                pool.wait_ge(multiplied, it * NG + (q + 1))
                                pool.sem_inc(begun, 1)
                                for i in range(G):
                                    nc.gpsimd.indirect_dma_start(
                                        rows[:, q, i, :], None, table_of,
                                        bass.IndirectOffsetOnAxis(ap=idx[:, q, i:i + 1], axis=0)).then_inc(gathered[q], 16)

                    @block.tensor
                    def _(pe):
                        pe.sem_inc(turned, 1)
                        pe.sem_inc(expanded, NG)

                        def turn(it, k):
                            pe.wait_ge(scored, it * NG + (2 * k + 3))
                            pe.wait_ge(copied, it * 2 + (k + 1))
                            nc.tensor.transpose(pT[k][0:10 * H, 0:P], sc[:, k * 10:(k + 1) * 10, :].rearrange("p t h -> p (t h)"),
                                                ident[:, :]).then_inc(turned, 1)

                        with pe.Fori(0, ITER) as it:
                            for q in range(NG):
                                own = owners(pe, own_d, it, q, NT)
                                pe.wait_ge(oht_made, it * NG + (NG + q + 1))
                                pe.wait_ge(multiplied, it * NG + (NG + q - 1))
                                for i in range(G):
                                    ins = nc.tensor.matmul(pE[q % 2][:, i * width:(i + 1) * width], oht[:, q, i * P:(i + 1) * P],
                                                           table[:, bass.ds(own[i], 1), 0:width], start=True, stop=True)
                                ins.then_inc(expanded, 1)
                                if q == 2:
                                    turn(it, 0)
                            turn(it, 1)

                    @block.scalar
                    def _(act):
                        act.sem_inc(copied, 1)
                        for k in range(2):
                            act.sem_inc(stored[k], 1)
                        with act.Fori(0, ITER) as it:
                            for k in range(2):
                                act.wait_ge(turned, it * 2 + (k + 2))
                                act.wait_ge(stored[k], it * 16 + 1)
                                nc.scalar.activation(srow[:, k, :], pT[k][0:10 * H, 0:P], ACT.Copy).then_inc(copied, 1)
                                act.wait_ge(copied, it * 2 + (k + 2))
                                act.dma_start(score_rows[bass.ds((it * T + k * 10) * H, 10 * H), :], srow[:, k, :]
                                              ).then_inc(stored[k], 16)
                        for k in range(2):
                            act.wait_ge(stored[k], ITER * 16 + 1)

                    @block.vector
                    def _(dve):
                        v = nc.vector
                        dve.sem_inc(oht_made, NG)
                        dve.sem_inc(multiplied, NG)
                        dve.sem_inc(scored, 1)
                        for q in range(NG):
                            v.tensor_copy(idx[:, q, :], src_idx[:, q * G:(q + 1) * G]).then_inc(idx_made, 1)

                        def head_sums(it, q):
                            dve.wait_ge(multiplied, it * NG + (NG + q + 1))
                            v.tensor_reduce(sc[:, q * G:(q + 1) * G, :], prod[:, q % 2, :, :].rearrange("p g (h d) -> p g h d", h=H),
                                            AX.X, ALU.add).then_inc(scored, 1)

                        with dve.Fori(0, ITER) as it:
                            for q in range(NG):
                                dve.wait_ge(bl_in[q], it * 16 + 16)
                                dve.wait_ge(expanded, it * NG + (q + 1))
                                v.tensor_scalar(oht[:, q, :], bl[:, q, :], iota_p[0:NP, :], None,
                                                ALU.is_equal).then_inc(oht_made, 1)
                            for q in range(NG):
                                if q == 0:
                                    dve.wait_ge(turned, it * 2 + 1)
                                if dots and q:
                                    head_sums(it, q - 1)
                                dve.wait_ge(gathered[q], it * (16 * G) + 16 * G)
                                dve.wait_ge(expanded, it * NG + (NG + q + 1))
                                e = pE[q % 2][:, 0:G * width].rearrange("p (g f) -> p g f", g=G)
                                v.tensor_copy(idx[:, q, :], src_idx[:, bass.ds(it * T + (T + q * G), G)]).then_inc(idx_made, 1)
                                if dots:
                                    dve.wait_ge(scored, it * NG + (q or 1))
                                    v.tensor_tensor(prod[:, q % 2, :, :], rows[:, q, :, :], e, ALU.mult).then_inc(multiplied, 1)
                                else:
                                    v.tensor_tensor(sc[:, q * G:(q + 1) * G, :], rows[:, q, :, :], e, ALU.add
                                                    ).then_inc(multiplied, 1)
                                    dve.wait_ge(multiplied, it * NG + (NG + q + 1))
                                    dve.sem_inc(scored, 1)
                            if dots:
                                head_sums(it, NG - 1)

        def softmax(tag, floor_zero, slope, scale):
            with ExitStack() as c:
                s, m = sb(c, tag + "s", [P, CE]), sb(c, tag + "m", [P, CE])
                seq = sb(c, tag + "seq", [P, CE + 2])
                mask = sb(c, tag + "mask", [P, CE])
                ends = sb(c, tag + "ends", [P, 4])
                row = sb(c, tag + "row", [1, 4, P])
                enter = sb(c, tag + "enter", [P, 2])
                pR = ps(c, tag + "pR", [P, 512])
                pC = ps(c, tag + "pC", [P, 512])
                s_in, s_pe, s_ch, s_e, s_p, s_out = (sem(c, tag + n) for n in "s_in s_pe s_ch s_e s_p s_out".split())
                by_head = score_rows.rearrange("(c t h) p -> h c t p", c=CH, t=CT, h=H)
                to_head = prob_rows.rearrange("(c t h) p -> h c t p", c=CH, t=CT, h=H)
                def load(eng, heads):
                    for h in heads:
                        rows = slice(h * CH, (h + 1) * CH)
                        eng.dma_start(s[rows, :].rearrange("c (t p) -> c t p", p=P), by_head[h]).then_inc(s_in, 16)
                        for a, b in ((0, CE), (CE, CE + 2)):
                            at = dst_seq[P - 1 + a:P - 1 + a + SQ * P].rearrange("(c e) -> c e", c=CH)
                            eng.dma_start(seq[rows, a:b], at[:, 0:b - a]).then_inc(s_in, 16)

                def store(eng, heads):
                    for h in heads:
                        eng.dma_start(to_head[h], s[h * CH:(h + 1) * CH, :].rearrange("c (t p) -> c t p", p=P)).then_inc(s_out, 16)

                with nc.Block() as block:
                    @block.sync
                    def _(sp):
                        load(sp, range(0, H, 2))
                        sp.wait_ge(s_p, 1)
                        store(sp, range(0, H, 2))
                        sp.wait_ge(s_out, 16 * H)

                    @block.tensor
                    def _(pe):
                        for d in range(2):
                            pe.wait_ge(s_e, 2 * d + 1)
                            for k in range(2):
                                ins = nc.tensor.transpose(pR[0:1, k * P:(k + 1) * P], ends[:, 2 * d + k:2 * d + k + 1], ident[:, :])
                            ins.then_inc(s_pe, 1)
                            pe.wait_ge(s_e, 2 * d + 2)
                            nc.tensor.transpose(pC[:, d:d + 1], row[:, 3, :], ident[0:1, 0:1]).then_inc(s_pe, 1)

                    @block.vector
                    def _(dve):
                        v = nc.vector
                        go = Link(dve, s_ch)
                        dve.wait_ge(s_in, 16 * 3 * H)
                        if floor_zero:
                            go(v.tensor_scalar(s[:, :], s[:, :], scale, None, ALU.mult))
                        else:
                            go(v.scalar_tensor_tensor(out=s[:, :], in0=s[:, :], scalar=slope, in1=s[:, :],
                                                      op0=ALU.mult, op1=ALU.max))
                        for d in range(2):
                            go(v.tensor_tensor(mask[:, :], seq[:, 1:CE + 1], seq[:, 2 * d:CE + 2 * d], ALU.not_equal))
                            go(v.tensor_scalar(mask[:, :], mask[:, :], -BIG, None, ALU.mult))
                            back = (lambda a: a[:, ::-1]) if d else (lambda a: a[:, :])
                            of = m if d else s
                            end = 0 if d else CE - 1
                            go(v.tensor_tensor_scan(back(m), back(mask), back(of), -BIG, ALU.add, ALU.max))
                            go(v.tensor_copy(ends[:, 2 * d:2 * d + 1], m[:, end:end + 1]))
                            v.tensor_reduce(ends[:, 2 * d + 1:2 * d + 2], mask[:, :], AX.X, ALU.min).then_inc(s_e, 1)
                            dve.wait_ge(s_pe, 2 * d + 1)
                            go(v.tensor_copy(row[:, 0, :], pR[0:1, 0:P]))
                            go(v.tensor_copy(row[:, 1, :], pR[0:1, P:2 * P]))
                            turn = (lambda a: a[:, ::-1]) if d else (lambda a: a)
                            go(v.tensor_tensor_scan(turn(row[:, 2, :]), turn(row[:, 1, :]), turn(row[:, 0, :]), -BIG,
                                                    ALU.add, ALU.max))
                            go(v.memset(row[:, 3, :], -BIG))
                            if d:
                                go(v.tensor_copy(row[:, 3, 0:P - 1], row[:, 2, 1:P]))
                            else:
                                go(v.tensor_copy(row[:, 3, 1:P], row[:, 2, 0:P - 1]))
                            v.memset(row[:, 0, :], 0.0).then_inc(s_e, 1)
                            dve.wait_ge(s_pe, 2 * d + 2)
                            go(v.tensor_copy(enter[:, d:d + 1], pC[:, d:d + 1]))
                            if d:
                                go(v.tensor_tensor_scan(back(m), back(mask), back(m), enter[:, d:d + 1], ALU.add, ALU.max))
                            else:
                                go(v.tensor_tensor_scan(m[:, :], mask[:, :], s[:, :], enter[:, d:d + 1], ALU.add, ALU.max))
                        if floor_zero:
                            go(v.tensor_scalar(m[:, :], m[:, :], 0.0, None, ALU.max))
                        v.tensor_tensor(s[:, :], s[:, :], m[:, :], ALU.subtract).then_inc(s_e, 1)

                    @block.scalar
                    def _(act):
                        load(act, range(1, H, 2))
                        act.wait_ge(s_e, 5)
                        nc.scalar.activation(s[:, :], s[:, :], ACT.Exp).then_inc(s_p, 1)
                        act.wait_ge(s_p, 1)
                        store(act, range(1, H, 2))

        def divide_by_weights(dve, sem_done, add, least):
            v, go = nc.vector, Link(dve, sem_done)
            den = acc[:, :, D:MW]
            go(v.tensor_scalar(den, den, add, least, ALU.add, ALU.max))
            go(v.reciprocal(den, den))
            for h in range(H):
                a = acc[:, :, h * DH:(h + 1) * DH]
                v.tensor_tensor(a, a, acc[:, :, D + h:D + h + 1].to_broadcast([NP, NTP, DH]), ALU.mult).then_inc(sem_done, 1)
            dve.wait_ge(sem_done, 2 + H)

        def normalise(tag, to, of, func, gain=None, shift=None, total=None, divide_sums=False, loads=()):
            cuts = [(t, min(t + 7, NTP)) for t in range(0, NTP, 7)]
            with ExitStack() as c:
                s_n, s_ch, s_m, s_g, s_l = (sem(c, tag + n) for n in "n ch m g l".split())
                with nc.Block() as block:
                    if loads:
                        @block.sync
                        def _(sp):
                            for place, from_ in loads:
                                sp.dma_start(place, from_).then_inc(s_l, 16)
                            sp.wait_ge(s_l, 16 * len(loads))

                    @block.scalar
                    def _(act):
                        for t in range(NTP):
                            nc.scalar.activation(to[:, t, 0:D], of[:, t, 0:D], func, bias=nmr[:, t:t + 1],
                                                 scale=rstd[:, t:t + 1]).then_inc(s_n, 1)

                    @block.vector
                    def _(dve):
                        v = nc.vector
                        if divide_sums:
                            divide_by_weights(dve, s_ch, 1e-8, 0.0)
                        if gain is not None:
                            for i, (a, b) in enumerate(cuts):
                                wide = [NP, b - a, D]
                                dve.wait_ge(s_n, b)
                                v.tensor_tensor(to[:, a:b, :], to[:, a:b, :], gain[0:NP, :].unsqueeze(1).to_broadcast(wide),
                                                ALU.mult).then_inc(s_m, 1)
                                dve.wait_ge(s_m, i + 1)
                                v.tensor_tensor(to[:, a:b, :], to[:, a:b, :], shift[0:NP, :].unsqueeze(1).to_broadcast(wide),
                                                ALU.add).then_inc(s_g, 1)
                                if total is not None:
                                    dve.wait_ge(s_g, i + 1)
                                    v.tensor_tensor(total[:, a:b, :], total[:, a:b, :], to[:, a:b, :], ALU.add)

        def feed_forward(w1, w2, b1, b2):
            F = 4
            with ExitStack() as c:
                uT = sb(c, "uT", [P, 2, 2, NP])
                gT = sb(c, "gT", [P, 2, F, NP])
                u = sb(c, "u", [NP, 2, D])
                pT = [ps(c, f"ffT{s}", [P, 2, 256]) for s in range(2)]
                pH = [ps(c, f"ffH{s}", [P, F, P]) for s in range(2)]
                pO = [ps(c, f"ffO{s}", [P, 512]) for s in range(2)]
                s_b = sem(c, "ff_b")
                s_u, s_t, s_c, s_h, s_g, s_o, s_a = ([sem(c, f"ff_{n}{s}") for s in range(2)]
                                                     for n in "u t c h g o a".split())
                with nc.Block() as block:
                    @block.tensor
                    def _(pe):
                        for s in range(2):
                            for counted in (s_t[s], s_h[s], s_o[s]):
                                pe.sem_inc(counted, 1)
                        with pe.Fori(0, NTP // 2) as it:
                            for s in range(2):
                                pe.wait_ge(s_u[s], it + 1)
                                pe.wait_ge(s_c[s], it + 1)
                                for k in range(2):
                                    ins = nc.tensor.transpose(pT[s][:, k, 0:NP], u[:, s, k * P:(k + 1) * P], ident[0:NP, 0:NP])
                                ins.then_inc(s_t[s], 1)
                            for s in range(2):
                                pe.wait_ge(s_c[s], it + 2)
                                pe.wait_ge(s_g[s], it * F + 1)
                                for f in range(F):
                                    for k in range(2):
                                        ins = nc.tensor.matmul(pH[s][:, f, 0:NP], w1[:, k, f * P:(f + 1) * P], uT[:, s, k, :],
                                                               start=k == 0, stop=k == 1)
                                ins.then_inc(s_h[s], 1)
                            for s in range(2):
                                pe.wait_ge(s_g[s], it * F + (F + 1))
                                pe.wait_ge(s_a[s], it + 1)
                                for f in range(F):
                                    ins = nc.tensor.matmul(pO[s][0:NP, 0:D], gT[:, s, f, :], w2[:, f, :], start=f == 0, stop=f == F - 1)
                                ins.then_inc(s_o[s], 1)

                    @block.scalar
                    def _(act):
                        for s in range(2):
                            act.sem_inc(s_g[s], 1)
                        with act.Fori(0, NTP // 2) as it:
                            for s in range(2):
                                act.wait_ge(s_t[s], it + 1)
                                nc.scalar.activation(u[:, s, :], table[:, bass.ds(it * 2 + s, 1), :].rearrange("p t f -> p (t f)"),
                                                     ACT.Copy).then_inc(s_u[s], 1)
                            for s in range(2):
                                act.wait_ge(s_h[s], it + 2)
                                act.wait_ge(s_o[s], it + 1)
                                for f in range(F):
                                    nc.scalar.activation(gT[:, s, f, :], pH[s][:, f, 0:NP], ACT.Gelu,
                                                         bias=b1[:, f:f + 1]).then_inc(s_g[s], 1)

                    @block.vector
                    def _(dve):
                        for s in range(2):
                            dve.sem_inc(s_c[s], 1)
                            dve.sem_inc(s_a[s], 1)
                        with dve.Fori(0, NTP // 2) as it:
                            for s in range(2):
                                dve.wait_ge(s_t[s], it + 2)
                                dve.wait_ge(s_h[s], it + 1)
                                nc.vector.tensor_copy(uT[:, s, :, :], pT[s][:, :, 0:NP]).then_inc(s_c[s], 1)
                            for s in range(2):
                                at = table[:, bass.ds(it * 2 + s, 1), :]
                                nc.vector.tensor_tensor(at, at, b2[0:NP, :].unsqueeze(1), ALU.add).then_inc(s_b, 1)
                            for s in range(2):
                                dve.wait_ge(s_o[s], it + 2)
                                dve.wait_ge(s_b, it * 2 + (s + 1))
                                at = table[:, bass.ds(it * 2 + s, 1), :]
                                nc.vector.tensor_tensor(at, at, pO[s][0:NP, 0:D].unsqueeze(1), ALU.add).then_inc(s_a[s], 1)

        def transformer_rest():
            with ExitStack() as c:
                wo = sb(c, "wo", [P, 2, D])
                vecs = sb(c, "vecs", [P, 6, D])
                w1 = sb(c, "w1f", [P, 2, 2 * D])
                w2 = sb(c, "w2f", [P, 4, D])
                b1 = sb(c, "b1f", [P, 4])
                loads = ([(wo[:, :, :], L2_gnn_Wo_w.rearrange("(k p) n -> p k n", p=P)),
                                  (w1[:, :, :], L2_gnn_ffn_w1.rearrange("(k p) n -> p k n", p=P)),
                                  (w2[:, :, :], L2_gnn_ffn_w2.rearrange("(k p) n -> p k n", p=P))]
                        + [(b1[:, f:f + 1], L2_gnn_ffn_b1[f * P:(f + 1) * P].rearrange("(p o) -> p o", o=1)) for f in range(4)]
                        + [(vecs[:, i, :], a.partition_broadcast(P)) for i, a in enumerate(
                            (L2_gnn_Wo_b, L2_gnn_ln1_g, L2_gnn_ln1_b, L2_gnn_ffn_b2, L2_gnn_ln2_g, L2_gnn_ln2_b))])
                normalise("n2", table, X, ACT.Relu, divide_sums=True, loads=loads)

                s_b = sem(c, "biased")

                def put(who, eng, it, s, pO, made, taken, stored):
                    if who == "dve":
                        at = table[:, bass.ds(it * 2 + s, 1), :]
                        nc.vector.tensor_tensor(at, at, vecs[0:NP, 0, :].unsqueeze(1), ALU.add).then_inc(s_b, 1)
                        eng.wait_ge(made[s], it + 2)
                        eng.wait_ge(s_b, it * 2 + (s + 1))
                        nc.vector.tensor_tensor(at, at, pO[s][0:NP, 0:D].unsqueeze(1), ALU.add).then_inc(taken[s], 1)
                project("dO", whole(wo), D, 1, put, copies=1, rows=acc)
                moments(table, "m1", clear_sums=True)
                normalise("n3", table, table, ACT.Identity, vecs[:, 1, :], vecs[:, 2, :])
                feed_forward(w1, w2, b1, vecs[:, 3, :])
                moments(table, "m2")
                normalise("n4", table, table, ACT.Identity, vecs[:, 4, :], vecs[:, 5, :], total=X)

        def last_layer_out():
            with ExitStack() as c:
                s_o, s_ch, s_a = sem(c, "written"), sem(c, "out_ch"), sem(c, "out_a")
                cuts = [(0, 9), (9, 17), (17, NT)]
                with nc.Block() as block:
                    @block.vector
                    def _(dve):
                        divide_by_weights(dve, s_ch, 0.0, 1e-30)
                        for a, b in cuts:
                            nc.vector.tensor_tensor(X[:, a:b, :], X[:, a:b, :], acc[:, a:b, 0:D], ALU.add).then_inc(s_a, 1)

                    @block.sync
                    def _(sp):
                        for i, (a, b) in enumerate(cuts):
                            sp.wait_ge(s_a, i + 1)
                            sp.dma_start(out[a * NP:b * NP, :].rearrange("(t p) f -> p t f", p=NP), X[:, a:b, :]).then_inc(s_o, 16)
                        sp.wait_ge(s_o, 16 * len(cuts))

        stages = [constants_and_edges,
                  scatter_by_source,
                  lambda: sum_over_edges("g0", own_s),
                  layer1_in, lambda: sum_over_edges("g1", own_d, (rel_table, rel_idx), weighted=True),
                  layer2_in, lambda: scores("c2", key_table, D), lambda: softmax("f2", True, None, SCALE),
                  lambda: sum_over_edges("g2", own_d, (value_table, src_idx), probs=True), transformer_rest,
                  layer3_in, lambda: scores("c3", s1_table, H), lambda: softmax("f3", False, 0.2, None),
                  lambda: sum_over_edges("g3", own_d, (wh_table, src_idx), probs=True), last_layer_out]
        for run in stages:
            run()


_INS = ['x', 'src', 'dst', 'edge_type_8', 'edge_weight', 'L0_gnn_weight', 'L1_gnn_weight', 'L2_gnn_Wq', 'L2_gnn_Wk',
        'L2_gnn_Wv', 'L2_gnn_Wo_w', 'L2_gnn_Wo_b', 'L2_gnn_ln1_g', 'L2_gnn_ln1_b', 'L2_gnn_ln2_g', 'L2_gnn_ln2_b',
        'L2_gnn_ffn_w1', 'L2_gnn_ffn_b1', 'L2_gnn_ffn_w2', 'L2_gnn_ffn_b2', 'L3_gnn_W', 'L3_gnn_a']


def kernel(**inputs):
    import numpy as _np
    import concourse.bacc as _bacc
    from concourse import mybir as _mybir
    from concourse.bass_utils import run_bass_kernel_spmd as _run

    nc = _bacc.Bacc("TRN2", target_bir_lowering=False, num_devices=1)
    arrays, args = {}, []
    for name in _INS:
        a = _np.ascontiguousarray(inputs[name])
        arrays[f"in_{name}"] = a
        args.append(nc.dram_tensor(f"in_{name}", a.shape, _mybir.dt.from_np(a.dtype), kind="ExternalInput").ap())
    args.append(nc.dram_tensor("out_x", (N, D), _mybir.dt.float32, kind="ExternalOutput").ap())
    build(nc, *args)
    r = _run(nc, [arrays], core_ids=[0])
    return r.results[0]["out_x"]
```
